# Optimizing a Trainium2 kernel written in Bass

```python
import numpy as np
import jax
import jax.numpy as jnp

def _softmax(x, axis=-1):
    return jax.nn.softmax(x, axis=axis)

def _gelu(x):
    return jax.nn.gelu(x, approximate=True)

def _silu(x):
    return jax.nn.silu(x)

def _sigmoid(x):
    return jax.nn.sigmoid(x)

def _layernorm(x, axis=-1, eps=1e-05):
    m = jnp.mean(x, axis=axis, keepdims=True)
    v = jnp.var(x, axis=axis, keepdims=True)
    return (x - m) / jnp.sqrt(v + eps)

def _scatter_add(tgt, idx, src, axis=0):
    return tgt.at[idx].add(src)

def _segment_sum(src, seg, n):
    return jax.ops.segment_sum(src, seg, n)
kernel_name = 'mk_xattn_ffn_d1_seqx_r8_4abb95'

def setup_inputs(seed: int=0):
    np.random.seed(seed)
    _w = jnp.asarray

    def _rec_inputs():
        import jax
        import jax.numpy as jnp
        _rk = jax.random.key(seed)
        x = 0.0003765 + 1 * jax.random.normal(jax.random.fold_in(_rk, 1), (8, 128, 256), jnp.float32)
        _lenS = 128 - jax.random.randint(jax.random.fold_in(_rk, 7), (8,), 0, max(1, 128 // 4) + 1, jnp.int32)
        _lenS2 = 128 - jax.random.randint(jax.random.fold_in(_rk, 8), (8,), 0, max(1, 128 // 4) + 1, jnp.int32)
        _ctx_2048P = jax.random.normal(jax.random.fold_in(_rk, 11), (8, 16, 256), jnp.float32)
        _ctx_2048c = jax.random.dirichlet(jax.random.fold_in(_rk, 511), 0.3 * jnp.ones((16,), jnp.float32), (8, 128))
        _ctx_2048t = jnp.einsum('bsk,bkd->bsd', _ctx_2048c, _ctx_2048P)
        _ctx_2048t = _ctx_2048t * jax.lax.rsqrt(jnp.mean(jnp.square(_ctx_2048t)) + 1e-12) * 0.953939
        ctx_2048 = -0.000292821 + 1.00034 * (_ctx_2048t + 0.3 * jax.random.normal(jax.random.fold_in(_rk, 611), (8, 128, 256), jnp.float32))
        return (x, ctx_2048)
    x, ctx_2048 = _rec_inputs()

    def _L0_xattn_setup():
        import jax, jax.numpy as jnp
        import numpy as np
        key = jax.random.key(seed)
        k1, k2, k3, k4, k5 = jax.random.split(key, 5)
        B, D_MODEL, L = (2, 128, 256)
        HEAD_DIM = 8
        H = D_MODEL // HEAD_DIM
        return {'k': jax.random.normal(k1, (B, D_MODEL, L), dtype=jnp.float32), 'v': jax.random.normal(k2, (B, D_MODEL, L), dtype=jnp.float32), 'q': jax.random.normal(k3, (B, D_MODEL, L), dtype=jnp.float32), 'ssm_kernel': jax.random.normal(k4, (H, L), dtype=jnp.float32), 'D': jax.random.normal(k5, (H,), dtype=jnp.float32), 'head_dim': HEAD_DIM}
    _L0_xattn_all = _L0_xattn_setup()
    _L0_xattn_in = {k: v for k, v in _L0_xattn_all.items() if k in ('ssm_kernel', 'D')}
    del _L0_xattn_all

    def _L0_ffn_setup():
        import jax, jax.numpy as jnp
        import numpy as np
        H, F, E, K = (256, 128, 16, 4)
        ROUTED_SCALE = 1.0
        key = jax.random.key(seed)
        ks = jax.random.split(key, 9)
        s = 0.02
        return {'x': jax.random.normal(ks[0], (4, 64, H), jnp.float32), 'router_w': jax.random.normal(ks[1], (E, H), jnp.float32) * s, 'router_bias': jnp.zeros((E,), jnp.float32), 'expert_gate_w': jax.random.normal(ks[2], (E, F, H), jnp.float32) * s, 'expert_up_w': jax.random.normal(ks[3], (E, F, H), jnp.float32) * s, 'expert_down_w': jax.random.normal(ks[4], (E, H, F), jnp.float32) * s, 'shared_gate_w': jax.random.normal(ks[5], (F, H), jnp.float32) * s, 'shared_up_w': jax.random.normal(ks[6], (F, H), jnp.float32) * s, 'shared_down_w': jax.random.normal(ks[7], (H, F), jnp.float32) * s}
    _L0_ffn_all = _L0_ffn_setup()
    _L0_ffn_in = {k: v for k, v in _L0_ffn_all.items() if k in ('router_w', 'router_bias', 'expert_gate_w', 'expert_up_w', 'expert_down_w', 'shared_gate_w', 'shared_up_w', 'shared_down_w')}
    del _L0_ffn_all
    return {'x': x, 'ctx_2048': ctx_2048, 'L0_xattn_ssm_kernel': _L0_xattn_in['ssm_kernel'], 'L0_xattn_D': _L0_xattn_in['D'], 'L0_ffn_router_w': _L0_ffn_in['router_w'], 'L0_ffn_router_bias': _L0_ffn_in['router_bias'], 'L0_ffn_expert_gate_w': _L0_ffn_in['expert_gate_w'], 'L0_ffn_expert_up_w': _L0_ffn_in['expert_up_w'], 'L0_ffn_expert_down_w': _L0_ffn_in['expert_down_w'], 'L0_ffn_shared_gate_w': _L0_ffn_in['shared_gate_w'], 'L0_ffn_shared_up_w': _L0_ffn_in['shared_up_w'], 'L0_ffn_shared_down_w': _L0_ffn_in['shared_down_w']}

def reference(x, ctx_2048, L0_xattn_ssm_kernel, L0_xattn_D, L0_ffn_router_w, L0_ffn_router_bias, L0_ffn_expert_gate_w, L0_ffn_expert_up_w, L0_ffn_expert_down_w, L0_ffn_shared_gate_w, L0_ffn_shared_up_w, L0_ffn_shared_down_w):
    import jax
    import jax.numpy as jnp

    def _L0_xattn_ref(k, v, q, ssm_kernel, D, head_dim):
        import jax, jax.numpy as jnp
        import numpy as np
        B, HD, L = k.shape
        H = HD // head_dim
        fft_size = 2 * L
        k_ = k.reshape(B, H, head_dim, L)
        v_ = v.reshape(B, H, head_dim, L)
        q_ = q.reshape(B, H, head_dim, L)
        kv = jnp.einsum('bhil,bhjl->bijhl', k_, v_)
        kv_f = jnp.fft.rfft(kv, n=fft_size)
        kernel_f = jnp.fft.rfft(ssm_kernel, n=fft_size)
        y = jnp.fft.irfft(kv_f * kernel_f, n=fft_size)[..., :L]
        out = y + kv * D[None, None, None, :, None]
        out = jnp.einsum('bijhl,bhil->bjhl', out, q_)
        out = jnp.transpose(out, (0, 2, 1, 3)).reshape(B, H * head_dim, L)
        return out.astype(k.dtype)

    def _L0_ffn_ref(x, router_w, router_bias, expert_gate_w, expert_up_w, expert_down_w, shared_gate_w, shared_up_w, shared_down_w):
        import jax, jax.numpy as jnp
        import numpy as np
        H, F, E, K = (256, 128, 16, 4)
        ROUTED_SCALE = 1.0
        orig_shape = x.shape
        h = x.reshape(-1, orig_shape[-1])
        T = h.shape[0]
        logits = h @ router_w.T
        scores = jax.nn.sigmoid(logits)
        choice = scores + router_bias[None, :]
        _, topk_idx = jax.lax.top_k(choice, K)
        topk_w = jnp.take_along_axis(scores, topk_idx, axis=1)
        topk_w = topk_w / (topk_w.sum(-1, keepdims=True) + 1e-20)
        topk_w = topk_w * ROUTED_SCALE
        comb = jnp.zeros((T, E), h.dtype).at[jnp.arange(T)[:, None], topk_idx].set(topk_w)
        g = jnp.einsum('th,efh->tef', h, expert_gate_w)
        u = jnp.einsum('th,efh->tef', h, expert_up_w)
        a = jax.nn.silu(g) * u
        routed = jnp.einsum('tef,te,ehf->th', a, comb, expert_down_w)
        shared = jax.nn.silu(h @ shared_gate_w.T) * (h @ shared_up_w.T) @ shared_down_w.T
        return (routed + shared).reshape(orig_shape)
    x = x + _L0_xattn_ref(ctx_2048, ctx_2048, _layernorm(x, axis=-1), L0_xattn_ssm_kernel, L0_xattn_D, 8)
    x = x + _L0_ffn_ref(_layernorm(x, axis=-1), L0_ffn_router_w, L0_ffn_router_bias, L0_ffn_expert_gate_w, L0_ffn_expert_up_w, L0_ffn_expert_down_w, L0_ffn_shared_gate_w, L0_ffn_shared_up_w, L0_ffn_shared_down_w)
    return x

_drawn_inputs = setup_inputs


def setup_inputs(seed=0):
    import zlib

    import numpy as np

    out = dict(_drawn_inputs(seed))
    spreads = {'L0_ffn_router_bias': (0.0, 0.8)}
    factors = {'L0_ffn_router_w': 8.0,
     'L0_ffn_expert_gate_w': 8.0,
     'L0_ffn_expert_up_w': 8.0,
     'L0_ffn_expert_down_w': 8.0,
     'L0_ffn_shared_gate_w': 8.0,
     'L0_ffn_shared_up_w': 8.0,
     'L0_ffn_shared_down_w': 8.0}
    for name, (base, spread) in spreads.items():
        noise = np.random.default_rng([zlib.crc32(name.encode()), seed]).standard_normal(out[name].shape)
        drawn = base * np.exp(spread * noise) if base else spread * noise
        out[name] = jnp.asarray(drawn.astype(out[name].dtype))
    for name, factor in factors.items():
        out[name] = (out[name] * factor).astype(out[name].dtype)
    return out
```

```python
from contextlib import ExitStack

import concourse.bass as bass
from concourse import mybir
from concourse.alu_op_type import AluOpType as ALU

F32 = mybir.dt.float32
F32R = mybir.dt.float32r
ACT = mybir.ActivationFunctionType
AX_X = mybir.AxisListType.X

P = 128
B = 8
L = 256
CH = L // P
HEADS = 16
HD = 8
PAIRS = HD * (HD + 1) // 2
E = 16
TOPK = 4
F = 128
WE = 6 * P
GU = 4 * P
GROUPS = [3, 3, 2]
NG = len(GROUPS)
NBM = max(GROUPS)
B0 = [sum(GROUPS[:g]) for g in range(NG)]
STEPS = E + 1
HB = 4
BLOCKS = HEADS // HB
LOOP_E = 3
RING = 3
EPS = 1e-5
SENT = -3.0e38
TAKEN = -1.0e38
SCW = E + TOPK
PAIR_AT = [sum(HD - e for e in range(d)) for d in range(HD)]


def build(nc, kpad, dskip, ctx_t, x_nat, x_t, w_all, router_t, bias_rows, out_t):
    with ExitStack() as ctx:
        def sb(name, shape, dt=F32):
            return ctx.enter_context(nc.sbuf_tensor(name, shape, dt))

        def sem(name):
            return ctx.enter_context(nc.semaphore(name))

        krow = sb("krow", [HEADS, P + L])
        drow = sb("drow", [HEADS, 1])
        ctxT = sb("ctxT", [P, B * CH, P])
        xnat = sb("xnat", [P, B, L])
        x1T = sb("x1T", [P, B * CH, P])
        toep = sb("toep", [P, HEADS * L])
        toep_w = sb("toep_w", [P, HB, L])
        kv = sb("kv", [P, HEADS, NBM * CH * PAIRS])
        Y = sb("Y", [P, HEADS * NBM * CH * PAIRS])
        Z = sb("Z", [P, HD, NBM * CH * HB * HD])
        qT = sb("qT", [P, B * CH, P])
        wraw = sb("wraw", [P, STEPS * WE])
        whi = sb("whi", [P, RING, WE], F32R)
        wlo = sb("wlo", [P, RING, WE], F32R)
        hn = sb("hn", [P, NBM, L])
        NTM = NBM * P
        hhi = sb("hhi", [P, 2, CH, NTM], F32R)
        hlo = sb("hlo", [P, 2, CH, NTM], F32R)
        sg = sb("sg", [P, NTM])
        tw = sb("tw", [P, NTM])
        av = sb("av", [P, RING, NTM])
        ahi = sb("ahi", [P, RING, NTM], F32R)
        alo = sb("alo", [P, RING, NTM], F32R)
        ident = sb("ident", [P, P])
        selcol = sb("selcol", [P, E])
        sel = sb("sel", [P, RING, P], F32R)
        rraw = sb("rraw", [P, CH * E])
        rhi = sb("rhi", [P, CH * E], F32R)
        rlo = sb("rlo", [P, CH * E], F32R)
        bias = sb("bias", [P, E])
        stats = sb("stats", [P, B, 6])
        mv = sb("mv", [P, 2 * B, 2])
        veps = sb("veps", [P, 2 * B])
        mhalf = sb("mhalf", [P, B])
        rstd = sb("rstd", [P, 2 * B])
        nbias = sb("nbias", [P, 2 * B])
        score = sb("score", [P, NBM, E])
        choice = sb("choice", [P, NBM, SCW])
        left = sb("left", [P, NBM, SCW])
        top = sb("top", [P, NBM, 8])
        chosen = sb("chosen", [P, NBM, E])
        wts = sb("wts", [P, NBM, E])
        tot = sb("tot", [P, NBM])
        tinv = sb("tinv", [P, NBM])
        comb = sb("comb", [P, NBM, P], F32R)
        combT = sb("combT", [P, 2, NTM], F32R)

        acc = [ctx.enter_context(nc.psum_tensor(f"acc{c}", [P, 512], F32)) for c in range(CH)]
        G = ctx.enter_context(nc.psum_tensor("G", [P, 512], F32))
        U = ctx.enter_context(nc.psum_tensor("U", [P, 512], F32))
        CB = ctx.enter_context(nc.psum_tensor("CB", [P, 512], F32))
        C = [ctx.enter_context(nc.psum_tensor(f"C{i}", [P, 512], F32)) for i in range(3)]

        toep_dram = nc.dram_tensor("toep_rows", (HEADS, P + L), F32, kind="Internal")

        s_k = sem("kernel_rows_loaded")
        s_kd = sem("kernel_rows_with_d")
        s_kout = sem("kernel_rows_stored")
        s_toep = sem("toeplitz_loaded")
        s_ctx = [sem(f"ctx_loaded{g}") for g in range(NG)]
        s_x = [sem(f"x_loaded{g}") for g in range(NG)]
        s_xT = sem("xT_loaded")
        s_small = sem("router_loaded")
        s_w = [sem(f"weights_loaded{i}") for i in range(3)]
        s_const = sem("constants_ready")
        s_cstep = sem("constants_step")
        s_chain = sem("vector_chain")
        s_rhi = sem("router_hi")
        s_rlo = sem("router_lo")
        s_var = sem("variances_ready")
        s_rstd = sem("rstd_ready")
        s_nb = sem("norm_bias_ready")
        s_norm = sem("rows_normalised")
        s_qtp = sem("queries_transposed")
        s_q = sem("queries_ready")
        s_kv = sem("kv_ready")
        s_tw = sem("block_toeplitz_ready")
        s_conv = sem("convolved")
        s_y = sem("conv_evacuated")
        s_z = sem("terms_step")
        s_x1 = sem("attention_added")
        s_xn = sem("x1_transposed")
        s_htp = sem("h_transposed")
        s_hh = sem("h_hi")
        s_hl = sem("h_lo")
        s_lg = sem("logits_ready")
        s_sc = sem("scores_ready")
        s_cx = sem("combine_ready")
        s_ctp = sem("combine_transposed")
        s_comb = sem("combine_in_place")
        s_wgh = sem("gate_up_hi")
        s_wgl = sem("gate_up_lo")
        s_wdh = sem("down_hi")
        s_wdl = sem("down_lo")
        s_sel = sem("select_ready")
        s_g = sem("gate_ready")
        s_u = sem("up_ready")
        s_silu = sem("silu_ready")
        s_t = sem("weighted_silu_ready")
        s_a = sem("act_ready")
        s_ah = sem("act_hi")
        s_al = sem("act_lo")
        s_acc = sem("group_accumulated")
        s_res = sem("result_ready")
        s_out = sem("result_stored")

        kdram = toep_dram.ap()
        block = ctx.enter_context(nc.Block())

        def gsl(g):
            return slice(B0[g] * CH, (B0[g] + GROUPS[g]) * CH)

        def lncols(i):
            if i < 2:
                return (0, GROUPS[0]) if i == 0 else (GROUPS[0], B - GROUPS[0])
            return B + B0[i - 2], GROUPS[i - 2]

        def wcols(s, first, n):
            return wraw[:, bass.ds(s * WE + first, n)]

        @block.sync
        def _(sp):
            sp.dma_start(krow[:, :], kpad).then_inc(s_k, 16)
            sp.dma_start(drow[:, :], dskip).then_inc(s_k, 16)
            for g in range(NG):
                c0, c1 = B0[g] * CH, (B0[g] + GROUPS[g]) * CH
                sp.dma_start(xnat[:, B0[g]:B0[g] + GROUPS[g], :],
                             x_nat[B0[g]:B0[g] + GROUPS[g]].rearrange("b p l -> p b l")).then_inc(s_x[g], 16)
                sp.dma_start(ctxT[:, c0:c1, :], ctx_t[:, c0:c1, :]).then_inc(s_ctx[g], 16)
                if g == 0:
                    sp.wait_ge(s_kd, 1)
                    sp.dma_start(kdram, krow[:, :]).then_inc(s_kout, 16)
                    sp.wait_ge(s_kout, 16)
                    src = bass.AP(kdram.tensor, kdram.offset + 1, [[1, P], [P + L, HEADS], [1, L]])
                    sp.dma_start(toep[:, :].rearrange("p (h l) -> p h l", h=HEADS), src).then_inc(s_toep, 16)
                    sp.dma_start(x1T[:, :, :], x_t).then_inc(s_xT, 16)
                    sp.dma_start(rraw[:, :], router_t).then_inc(s_small, 16)
                    sp.dma_start(bias[:, :], bias_rows).then_inc(s_small, 16)
                    for i, (a, b) in enumerate(((0, 1), (1, 3), (3, STEPS))):
                        sp.dma_start(wraw[:, a * WE:b * WE], w_all[:, a * WE:b * WE]).then_inc(s_w[i], 16)
            for g in range(NG):
                sp.wait_ge(s_res, g + 1)
                sp.dma_start(out_t[:, gsl(g), :], x1T[:, gsl(g), :]).then_inc(s_out, 16)
            sp.wait_ge(s_out, 16 * NG)

        @block.gpsimd
        def _(pool):
            tt = nc.gpsimd.tensor_tensor

            def rsqrt(i):
                pool.wait_ge(s_var, i + 1)
                c, n = lncols(i)
                tt(rstd[:, c:c + n], veps[:, c:c + n], mhalf[:, 0:n], ALU.pow).then_inc(s_rstd, 1)

            def kv_block(g, k):
                x = ctxT[:, gsl(g), bass.ds(k * HB * HD, HB * HD)].rearrange("p c (h i) -> p h c i", i=HD)
                dst = kv[:, bass.ds(k * HB, HB), 0:GROUPS[g] * CH * PAIRS].rearrange("p h (c n) -> p h c n", n=PAIRS)
                for d in range(HD):
                    ins = tt(dst[:, :, :, PAIR_AT[d]:PAIR_AT[d] + HD - d], x[:, :, :, 0:HD - d],
                             x[:, :, :, d:HD], ALU.mult)
                ins.then_inc(s_kv, 1)

            def kv_first(g):
                pool.wait_ge(s_ctx[g], 16)
                if g:
                    pool.wait_ge(s_conv, 2 * BLOCKS * g)
                kv_block(g, 0)

            def gate_up_lo(n, r, s):
                pool.wait_ge(s_wgh, n + 1)
                tt(wlo[:, r, 0:GU], wcols(s, 0, GU), whi[:, r, 0:GU].bitcast(F32), ALU.subtract).then_inc(s_wgl, 1)

            def act_lo(g, n, r):
                pool.wait_ge(s_ah, n + 1)
                nt = GROUPS[g] * P
                tt(alo[:, r, 0:nt], av[:, r, 0:nt], ahi[:, r, 0:nt].bitcast(F32), ALU.subtract).then_inc(s_al, 1)

            nc.gpsimd.memset(mhalf[:, :], -0.5).then_inc(s_cstep, 1)
            nc.gpsimd.memset(ident[:, :], 0.0).then_inc(s_cstep, 1)
            nc.gpsimd.memset(selcol[:, :], 0.0).then_inc(s_cstep, 1)
            pool.wait_ge(s_cstep, 3)
            nc.gpsimd.affine_select(out=ident[:, :], in_=ident[:, :], compare_op=ALU.not_equal, fill=1.0,
                                    base=0, pattern=[[-1, P]], channel_multiplier=1).then_inc(s_const, 1)
            nc.gpsimd.affine_select(out=selcol[:, :], in_=selcol[:, :], compare_op=ALU.not_equal, fill=1.0,
                                    base=0, pattern=[[-1, E]], channel_multiplier=1).then_inc(s_cstep, 1)
            pool.wait_ge(s_cstep, 4)
            nc.gpsimd.affine_select(out=selcol[:, :], in_=selcol[:, :], compare_op=ALU.not_equal, fill=1.0,
                                    base=-E, pattern=[[-1, E]], channel_multiplier=1).then_inc(s_const, 1)
            kv_first(0)
            rsqrt(0)
            rsqrt(1)
            with pool.Fori(1, BLOCKS) as k:
                kv_block(0, k)
            for m in range(2):
                gate_up_lo(m, m, m)
            rsqrt(2)
            for g in range(NG):
                n0 = g * STEPS
                nxt = g + 1 < NG
                gate_up_lo(n0 + 2, (n0 + 2) % RING, 2)
                act_lo(g, n0, n0 % RING)
                if nxt:
                    kv_first(g + 1)
                with pool.Fori(0, BLOCKS - 1) as k:
                    for j in range(LOOP_E):
                        n = n0 + 1 + j
                        gate_up_lo(k * LOOP_E + (n + 2), (n + 2) % RING, k * LOOP_E + (3 + j))
                        act_lo(g, k * LOOP_E + n, n % RING)
                        if nxt and j == 0:
                            kv_block(g + 1, k + 1)
                for s in range(1 + LOOP_E * (BLOCKS - 1), STEPS):
                    n = n0 + s
                    if s + 2 < STEPS or nxt:
                        gate_up_lo(n + 2, (n + 2) % RING, (s + 2) % STEPS)
                    act_lo(g, n, n % RING)
                    if nxt and s == 13:
                        rsqrt(2 + g + 1)

        @block.scalar
        def _(act):
            def normalise(i, g, src):
                act.wait_ge(s_nb, i + 1)
                c = B0[g] + (B if i >= 2 else 0)
                for b in range(GROUPS[g]):
                    ins = nc.scalar.activation(hn[:, b, :], src(b), ACT.Identity, bias=nbias[:, c + b:c + b + 1],
                                               scale=rstd[:, c + b:c + b + 1])
                ins.then_inc(s_norm, 1)

            def queries(g):
                act.wait_ge(s_x[g], 16)
                normalise(min(g, 1), g, lambda b: xnat[:, B0[g] + b, :])
                act.wait_ge(s_qtp, g + 1)
                n = GROUPS[g]
                dst = qT[:, gsl(g), :].rearrange("p c n -> p (c n)")
                ins = nc.scalar.copy(dst[:, 0:min(n, 2) * L], C[0][:, 0:min(n, 2) * L])
                if n > 2:
                    ins = nc.scalar.copy(dst[:, 2 * L:n * L], C[1][:, 0:(n - 2) * L])
                ins.then_inc(s_q, 1)

            def block_toeplitz(k):
                nc.scalar.copy(toep_w[:, :, :].rearrange("p h l -> p (h l)"),
                               toep[:, bass.ds(k * HB * L, HB * L)]).then_inc(s_tw, 1)

            def evacuate(g, k):
                w = GROUPS[g] * CH * PAIRS
                for half in range(2):
                    act.wait_ge(s_conv, 2 * k + (2 * BLOCKS * g + half + 1))
                    nc.scalar.copy(Y[:, bass.ds(k * (HB * w) + 2 * half * w, 2 * w)],
                                   C[half][:, 0:2 * w]).then_inc(s_y, 1)

            def gate_up_hi(r, s):
                nc.scalar.copy(whi[:, r, 0:GU], wcols(s, 0, GU)).then_inc(s_wgh, 1)

            def down_hi(r, s):
                nc.scalar.copy(whi[:, r, GU:WE], wcols(s, GU, WE - GU)).then_inc(s_wdh, 1)

            def silu(g, n):
                act.wait_ge(s_g, n + 1)
                nt = GROUPS[g] * P
                nc.scalar.activation(sg[:, 0:nt], G[:, 0:nt], ACT.Silu).then_inc(s_silu, 1)

            def act_hi(g, n, r):
                act.wait_ge(s_a, n + 1)
                nt = GROUPS[g] * P
                nc.scalar.copy(ahi[:, r, 0:nt], av[:, r, 0:nt]).then_inc(s_ah, 1)

            def h_hi(g):
                act.wait_ge(s_htp, g + 1)
                nt = GROUPS[g] * P
                nc.scalar.copy(hhi[:, g % 2, 0, 0:nt], C[2][:, 0:nt]).then_inc(s_hh, 1)
                nc.scalar.copy(hhi[:, g % 2, 1, 0:nt], C[0][:, 0:nt]).then_inc(s_hh, 1)

            def x1_row(b):
                return C[b // 2][:, (b % 2) * L:(b % 2 + 1) * L]

            def scores(g):
                act.wait_ge(s_lg, g + 1)
                n = GROUPS[g]
                nc.scalar.activation(score[:, 0:n, :].rearrange("p b e -> p (b e)"), C[1][:, 0:n * E],
                                     ACT.Sigmoid).then_inc(s_sc, 1)

            def combine_in_place(g):
                act.wait_ge(s_ctp, g + 1)
                nt = GROUPS[g] * P
                nc.scalar.copy(combT[:, g % 2, 0:nt], C[2][:, 0:nt]).then_inc(s_comb, 1)

            act.wait_ge(s_small, 32)
            nc.scalar.copy(rhi[:, :], rraw[:, :]).then_inc(s_rhi, 1)
            queries(0)
            act.wait_ge(s_toep, 16)
            with act.Fori(0, BLOCKS) as k:
                block_toeplitz(k)
                evacuate(0, k)
            for g in range(1, NG):
                queries(g)
            act.wait_ge(s_w[0], 16)
            gate_up_hi(0, 0)
            down_hi(0, 0)
            act.wait_ge(s_w[1], 16)
            gate_up_hi(1, 1)
            normalise(2, 0, x1_row)
            h_hi(0)
            scores(0)
            combine_in_place(0)
            for g in range(NG):
                n0 = g * STEPS
                nxt = g + 1 < NG
                silu(g, n0)
                gate_up_hi((n0 + 2) % RING, 2)
                down_hi((n0 + 1) % RING, 1)
                act_hi(g, n0, n0 % RING)
                if g == 0:
                    act.wait_ge(s_w[2], 16)
                else:
                    combine_in_place(g)
                if nxt:
                    act.wait_ge(s_x1, BLOCKS * (g + 1))
                with act.Fori(0, BLOCKS) as k:
                    if nxt:
                        block_toeplitz(k)
                    for j in range(LOOP_E):
                        n = n0 + 1 + j
                        silu(g, k * LOOP_E + n)
                        gate_up_hi((n + 2) % RING, k * LOOP_E + (3 + j))
                        down_hi((n + 1) % RING, k * LOOP_E + (2 + j))
                        act_hi(g, k * LOOP_E + n, n % RING)
                        if nxt and j == 0:
                            evacuate(g + 1, k)
                for s in range(1 + LOOP_E * BLOCKS, STEPS):
                    n = n0 + s
                    silu(g, n)
                    if s + 2 < STEPS or nxt:
                        gate_up_hi((n + 2) % RING, (s + 2) % STEPS)
                    if s + 1 < STEPS or nxt:
                        down_hi((n + 1) % RING, (s + 1) % STEPS)
                    act_hi(g, n, n % RING)
                    if nxt and s == 14:
                        normalise(2 + g + 1, g + 1, x1_row)
                    if nxt and s == 15:
                        h_hi(g + 1)
                if nxt:
                    scores(g + 1)

        @block.vector
        def _(dve):
            tt = nc.vector.tensor_tensor
            chain = [0]

            def link(ins):
                chain[0] += 1
                ins.then_inc(s_chain, 1)
                dve.wait_ge(s_chain, chain[0])

            def statistics(i, rows):
                c, n = lncols(i)
                for b in range(n):
                    ins = nc.vector.bn_stats(stats[:, b, :], rows(b))
                link(ins)
                for b in range(n):
                    ins = nc.vector.bn_aggr(mv[:, c + b, :], stats[:, b, :])
                link(ins)
                nc.vector.tensor_scalar(veps[:, c:c + n], mv[:, c:c + n, 1], EPS, None,
                                        ALU.add).then_inc(s_var, 1)

            def norm_bias(i):
                dve.wait_ge(s_rstd, i + 1)
                c, n = lncols(i)
                nc.vector.scalar_tensor_tensor(out=nbias[:, c:c + n], in0=mv[:, c:c + n, 0], scalar=-1.0,
                                               in1=rstd[:, c:c + n], op0=ALU.mult, op1=ALU.mult).then_inc(s_nb, 1)

            def x1_row(b):
                return C[b // 2][:, (b % 2) * L:(b % 2 + 1) * L]

            TERMS = [(d, 0, d) for d in range(HD)] + [(HD - d, d, 0) for d in range(1, HD)]

            def terms(g, k, first, last):
                w = GROUPS[g] * CH * PAIRS
                y = Y[:, bass.ds(k * (HB * w), HB * w)].rearrange("p (h c n) -> p h c n", h=HB, n=PAIRS)
                q = qT[:, gsl(g), bass.ds(k * HB * HD, HB * HD)].rearrange("p c (h i) -> p h c i", i=HD)
                z = Z[:, :, 0:GROUPS[g] * CH * HB * HD].rearrange("p e (c h j) -> p e h c j", h=HB, j=HD)
                for e, qi, zj in TERMS[first:last]:
                    d = e if qi == 0 else qi
                    ins = tt(z[:, e, :, :, zj:zj + HD - d], y[:, :, :, PAIR_AT[d]:PAIR_AT[d] + HD - d],
                             q[:, :, :, qi:qi + HD - d], ALU.mult)
                return ins

            def add_terms(g, k, ins):
                w = GROUPS[g] * CH * HB * HD
                z0 = 4 * BLOCKS * g
                ins.then_inc(s_z, 1)
                for i, half in enumerate((4, 2, 1)):
                    dve.wait_ge(s_z, 4 * k + (z0 + i + 1))
                    tt(Z[:, 0:half, 0:w], Z[:, 0:half, 0:w], Z[:, half:2 * half, 0:w], ALU.add).then_inc(s_z, 1)
                dve.wait_ge(s_z, 4 * k + (z0 + 4))
                x = x1T[:, gsl(g), bass.ds(k * HB * HD, HB * HD)]
                tt(x, x, Z[:, 0, 0:w].rearrange("p (c n) -> p c n", n=HB * HD), ALU.add).then_inc(s_x1, 1)
                dve.wait_ge(s_x1, k + (BLOCKS * g + 1))

            def block_start(g, k):
                dve.wait_ge(s_y, 2 * k + 2 * BLOCKS * g + 2)

            def select(r, s):
                nc.vector.tensor_copy(sel[:, r, :], selcol[:, bass.ds(s - 1, 1)].to_broadcast([P, P])).then_inc(s_sel, 1)

            def down_lo(n, r, s):
                dve.wait_ge(s_wdh, n + 1)
                tt(wlo[:, r, GU:WE], wcols(s, GU, WE - GU), whi[:, r, GU:WE].bitcast(F32),
                   ALU.subtract).then_inc(s_wdl, 1)

            def activations(g, n, r, at):
                nt = GROUPS[g] * P
                dve.wait_ge(s_silu, n + 1)
                gate = sg
                if at is not None:
                    tt(tw[:, 0:nt], sg[:, 0:nt], CB[:, 0:nt], ALU.mult).then_inc(s_t, 1)
                    dve.wait_ge(s_t, at + 1)
                    gate = tw
                dve.wait_ge(s_u, n + 1)
                tt(av[:, r, 0:nt], gate[:, 0:nt], U[:, 0:nt], ALU.mult).then_inc(s_a, 1)

            def h_lo(g):
                nt = GROUPS[g] * P
                for c, src in enumerate((C[2], C[0])):
                    dve.wait_ge(s_hh, 2 * g + c + 1)
                    ins = tt(hlo[:, g % 2, c, 0:nt], src[:, 0:nt], hhi[:, g % 2, c, 0:nt].bitcast(F32),
                             ALU.subtract)
                ins.then_inc(s_hl, 1)

            def combine(g):
                n = GROUPS[g]
                dve.wait_ge(s_sc, g + 1)
                link(tt(choice[:, 0:n, 0:E], score[:, 0:n, :],
                        bias[:, :].unsqueeze(1).to_broadcast([P, n, E]), ALU.add))
                for b in range(n):
                    ins = nc.vector.max(top[:, b, :], choice[:, b, 0:E])
                link(ins)
                link(nc.vector.memset(top[:, 0:n, TOPK:8], SENT))
                for b in range(n):
                    ins = nc.vector.match_replace(out=left[:, b, :], in_to_replace=top[:, b, :],
                                                  in_values=choice[:, b, :], imm_value=TAKEN)
                link(ins)
                link(tt(chosen[:, 0:n, :], choice[:, 0:n, 0:E], left[:, 0:n, 0:E], ALU.not_equal))
                link(tt(wts[:, 0:n, :], score[:, 0:n, :], chosen[:, 0:n, :], ALU.mult))
                link(nc.vector.tensor_reduce(tot[:, 0:n], wts[:, 0:n, :], AX_X, ALU.add))
                link(nc.vector.tensor_scalar(tot[:, 0:n], tot[:, 0:n], 1e-20, None, ALU.add))
                link(nc.vector.reciprocal(tinv[:, 0:n], tot[:, 0:n]))
                link(tt(wts[:, 0:n, :], wts[:, 0:n, :], tinv[:, 0:n].unsqueeze(2).to_broadcast([P, n, E]), ALU.mult))
                link(nc.vector.tensor_copy(comb[:, 0:n, 0:E], wts[:, 0:n, :]))
                tt(comb[:, 0:n, E:2 * E], wts[:, 0:n, :], comb[:, 0:n, 0:E].bitcast(F32),
                   ALU.subtract).then_inc(s_cx, 1)

            def result(g):
                dve.wait_ge(s_acc, g + 1)
                n = GROUPS[g]
                x = x1T[:, gsl(g), :].rearrange("p (b c) n -> p b c n", c=CH)
                for c in range(CH):
                    ins = tt(x[:, :, c, :], acc[c][:, 0:n * P].rearrange("p (b n) -> p b n", n=P), x[:, :, c, :],
                             ALU.add)
                ins.then_inc(s_res, 1)

            dve.wait_ge(s_k, 32)
            tt(krow[:, P:P + 1], krow[:, P:P + 1], drow[:, :], ALU.add).then_inc(s_kd, 1)
            dve.wait_ge(s_x[0], 16)
            statistics(0, lambda b: xnat[:, b, :])
            nc.vector.memset(comb[:, :, :].bitcast(F32), 0.0)
            nc.vector.memset(choice[:, :, :], SENT)
            norm_bias(0)
            dve.wait_ge(s_rhi, 1)
            tt(rlo[:, :], rraw[:, :], rhi[:, :].bitcast(F32), ALU.subtract).then_inc(s_rlo, 1)
            for g in range(1, NG):
                dve.wait_ge(s_x[g], 16)
            statistics(1, lambda b: xnat[:, GROUPS[0] + b, :])
            norm_bias(1)
            dve.wait_ge(s_xT, 16)
            dve.wait_ge(s_q, 1)
            with dve.Fori(0, BLOCKS) as k:
                block_start(0, k)
                add_terms(0, k, terms(0, k, 0, len(TERMS)))
            dve.wait_ge(s_w[0], 16)
            down_lo(0, 0, 0)
            dve.wait_ge(s_xn, 1)
            statistics(2, x1_row)
            norm_bias(2)
            dve.wait_ge(s_const, 2)
            h_lo(0)
            combine(0)
            for g in range(NG):
                n0 = g * STEPS
                nxt = g + 1 < NG
                activations(g, n0, n0 % RING, None)
                select((n0 + 1) % RING, 1)
                down_lo(n0 + 1, (n0 + 1) % RING, 1)
                if g:
                    result(g - 1)
                if nxt:
                    dve.wait_ge(s_q, g + 2)
                with dve.Fori(0, BLOCKS) as k:
                    for j in range(LOOP_E):
                        n = n0 + 1 + j
                        activations(g, k * LOOP_E + n, n % RING, k * LOOP_E + (g * E + j))
                        select((n + 1) % RING, k * LOOP_E + (2 + j))
                        down_lo(k * LOOP_E + (n + 1), (n + 1) % RING, k * LOOP_E + (2 + j))
                        if nxt:
                            if j == 0:
                                block_start(g + 1, k)
                                terms(g + 1, k, 0, 6)
                            elif j == 1:
                                terms(g + 1, k, 6, 12)
                            else:
                                add_terms(g + 1, k, terms(g + 1, k, 12, len(TERMS)))
                for s in range(1 + LOOP_E * BLOCKS, STEPS):
                    n = n0 + s
                    activations(g, n, n % RING, g * E + s - 1)
                    if s + 1 < STEPS:
                        select((n + 1) % RING, s + 1)
                    if s + 1 < STEPS or nxt:
                        down_lo(n + 1, (n + 1) % RING, (s + 1) % STEPS)
                    if nxt and s == 13:
                        dve.wait_ge(s_xn, g + 2)
                        statistics(2 + g + 1, x1_row)
                    if nxt and s == 14:
                        norm_bias(2 + g + 1)
                    if nxt and s == 15:
                        h_lo(g + 1)
                if nxt:
                    combine(g + 1)
            result(NG - 1)

        @block.tensor
        def _(pe):
            mm = nc.tensor.matmul

            def queries(g):
                pe.wait_ge(s_norm, g + 1)
                for b in range(GROUPS[g]):
                    for c in range(CH):
                        at = (b % 2) * L + c * P
                        ins = nc.tensor.transpose(C[b // 2][:, at:at + P], hn[:, b, c * P:(c + 1) * P], ident[:, :])
                ins.then_inc(s_qtp, 1)

            def convolve(g, k):
                w = GROUPS[g] * CH * PAIRS
                pe.wait_ge(s_kv, k + (BLOCKS * g + 1))
                pe.wait_ge(s_tw, k + (BLOCKS * g + 1))
                for h in range(HB):
                    m = kv[:, bass.ds(k * HB + h, 1), 0:w].rearrange("p o (b c n) -> p (o b) c n", c=CH, n=PAIRS)
                    y = C[h // 2][:, (h % 2) * w:(h % 2 + 1) * w].rearrange("p (b c n) -> p b c n", c=CH, n=PAIRS)
                    near, far = toep_w[:, h, 0:P], toep_w[:, h, P:L]
                    mm(y[:, :, 0, :], near, m[:, :, 0, :], start=True, stop=True)
                    mm(y[:, :, 1, :], near, m[:, :, 1, :], start=True, stop=False)
                    ins = mm(y[:, :, 1, :], far, m[:, :, 0, :], start=False, stop=True)
                    if h % 2:
                        ins.then_inc(s_conv, 1)

            def x1_rows(g):
                pe.wait_ge(s_x1, BLOCKS * (g + 1))
                for b in range(GROUPS[g]):
                    for c in range(CH):
                        at = (b % 2) * L + c * P
                        ins = nc.tensor.transpose(C[b // 2][:, at:at + P], x1T[:, (B0[g] + b) * CH + c, :], ident[:, :])
                ins.then_inc(s_xn, 1)

            def h_turned(g):
                pe.wait_ge(s_norm, NG + g + 1)
                for c, dst in enumerate((C[2], C[0])):
                    for b in range(GROUPS[g]):
                        ins = nc.tensor.transpose(dst[:, b * P:(b + 1) * P], hn[:, b, c * P:(c + 1) * P], ident[:, :])
                ins.then_inc(s_htp, 1)

            def product3(out, whi_, wlo_, xhi, xlo, start, stop):
                mm(out, whi_, xhi, start=start, stop=False, skip_group_check=True)
                mm(out, whi_, xlo, start=False, stop=False, skip_group_check=True)
                return mm(out, wlo_, xhi, start=False, stop=stop, skip_group_check=True)

            def router(g):
                pe.wait_ge(s_hl, g + 1)
                for b in range(GROUPS[g]):
                    out = C[1][:, b * E:(b + 1) * E]
                    for c in range(CH):
                        h1, h2 = (t[:, g % 2, c, b * P:(b + 1) * P] for t in (hhi, hlo))
                        r1, r2 = (t[:, c * E:(c + 1) * E] for t in (rhi, rlo))
                        mm(out, h1, r1, start=(c == 0), stop=False)
                        mm(out, h1, r2, start=False, stop=False)
                        ins = mm(out, h2, r1, start=False, stop=(c == CH - 1))
                ins.then_inc(s_lg, 1)

            def combine_turned(g):
                pe.wait_ge(s_cx, g + 1)
                for b in range(GROUPS[g]):
                    ins = nc.tensor.transpose(C[2][:, b * P:(b + 1) * P], comb[:, b, :].bitcast(F32), ident[:, :])
                ins.then_inc(s_ctp, 1)

            def spread(g, n, r, s):
                nt = GROUPS[g] * P
                pe.wait_ge(s_a, n)
                pe.wait_ge(s_sel, g * E + s)
                mm(CB[:, 0:nt], sel[:, r, :], combT[:, g % 2, 0:nt], start=True, stop=True)

            def gate_up(g, n, r):
                nt = GROUPS[g] * P
                pe.wait_ge(s_wgl, n + 1)
                for half, (out, done) in enumerate(((G, s_g), (U, s_u))):
                    for c in range(CH):
                        at = (2 * half + c) * P
                        ins = product3(out[:, 0:nt], whi[:, r, at:at + P], wlo[:, r, at:at + P],
                                       hhi[:, g % 2, c, 0:nt], hlo[:, g % 2, c, 0:nt], c == 0, c == CH - 1)
                    ins.then_inc(done, 1)

            def down(g, n, r, first=False, last=False):
                nt = GROUPS[g] * P
                pe.wait_ge(s_al, n + 1)
                pe.wait_ge(s_wdl, n + 1)
                for c in range(CH):
                    at = GU + c * P
                    ins = product3(acc[c][:, 0:nt], whi[:, r, at:at + P], wlo[:, r, at:at + P],
                                   ahi[:, r, 0:nt], alo[:, r, 0:nt], first, last)
                if last:
                    ins.then_inc(s_acc, 1)

            pe.wait_ge(s_const, 2)
            queries(0)
            with pe.Fori(0, BLOCKS) as k:
                convolve(0, k)
            for g in range(1, NG):
                pe.wait_ge(s_q, g)
                queries(g)
            pe.wait_ge(s_q, NG)
            x1_rows(0)
            h_turned(0)
            pe.wait_ge(s_rlo, 1)
            router(0)
            for g in range(NG):
                n0 = g * STEPS
                nxt = g + 1 < NG
                if g:
                    pe.wait_ge(s_a, n0)
                gate_up(g, n0, n0 % RING)
                if g:
                    down(g - 1, n0 - 1, (n0 - 1) % RING, last=True)
                combine_turned(g)
                pe.wait_ge(s_comb, g + 1)
                spread(g, n0 + 1, (n0 + 1) % RING, 1)
                gate_up(g, n0 + 1, (n0 + 1) % RING)
                if g:
                    pe.wait_ge(s_res, g)
                down(g, n0, n0 % RING, first=True)
                with pe.Fori(0, BLOCKS) as k:
                    if nxt:
                        convolve(g + 1, k)
                    for j in range(LOOP_E):
                        n = n0 + 2 + j
                        spread(g, k * LOOP_E + n, n % RING, k * LOOP_E + (2 + j))
                        gate_up(g, k * LOOP_E + n, n % RING)
                        down(g, k * LOOP_E + (n - 1), (n - 1) % RING)
                if nxt:
                    x1_rows(g + 1)
                for s in range(2 + LOOP_E * BLOCKS, STEPS):
                    n = n0 + s
                    spread(g, n, n % RING, s)
                    gate_up(g, n, n % RING)
                    down(g, n - 1, (n - 1) % RING)
                    if nxt and s == 15:
                        h_turned(g + 1)
                if nxt:
                    router(g + 1)
            down(NG - 1, NG * STEPS - 1, (NG * STEPS - 1) % RING, last=True)


def kernel(x, ctx_2048, L0_xattn_ssm_kernel, L0_xattn_D, L0_ffn_router_w, L0_ffn_router_bias,
           L0_ffn_expert_gate_w, L0_ffn_expert_up_w, L0_ffn_expert_down_w, L0_ffn_shared_gate_w,
           L0_ffn_shared_up_w, L0_ffn_shared_down_w):
    import numpy as np
    import concourse.bacc as bacc
    from concourse.bass_utils import run_bass_kernel_spmd

    def positions_first(a):
        return np.ascontiguousarray(np.asarray(a).reshape(B, P, CH, P).transpose(3, 0, 2, 1).reshape(P, B * CH, P))

    def with_shared(shared, experts):
        return np.concatenate([np.asarray(shared)[None], np.asarray(experts)], 0)

    def in_first(w):
        return w.reshape(STEPS, F, CH, P).transpose(3, 0, 2, 1).reshape(P, STEPS, CH * F)

    xs = np.asarray(x)
    gate = in_first(with_shared(L0_ffn_shared_gate_w, L0_ffn_expert_gate_w))
    up = in_first(with_shared(L0_ffn_shared_up_w, L0_ffn_expert_up_w))
    down = with_shared(L0_ffn_shared_down_w, L0_ffn_expert_down_w).transpose(2, 0, 1)
    ker = np.asarray(L0_xattn_ssm_kernel)
    arrays = {
        "kernel_rows": np.ascontiguousarray(np.concatenate([np.zeros((HEADS, P), ker.dtype), ker], 1)),
        "d_skip": np.ascontiguousarray(np.asarray(L0_xattn_D).reshape(HEADS, 1)),
        "ctx_t": np.ascontiguousarray(positions_first(ctx_2048)[::-1]),
        "x_nat": np.ascontiguousarray(xs),
        "x_t": positions_first(xs),
        "w_all": np.ascontiguousarray(np.concatenate([gate, up, down], 2).reshape(P, STEPS * WE)),
        "router_t": np.ascontiguousarray(
            np.asarray(L0_ffn_router_w).reshape(E, CH, P).transpose(2, 1, 0).reshape(P, CH * E)),
        "bias_rows": np.ascontiguousarray(np.broadcast_to(np.asarray(L0_ffn_router_bias), (P, E))),
    }
    nc = bacc.Bacc("TRN2", target_bir_lowering=False, num_devices=1)
    args = [nc.dram_tensor(name, a.shape, mybir.dt.from_np(a.dtype), kind="ExternalInput").ap()
            for name, a in arrays.items()]
    out = nc.dram_tensor("out_t", (P, B * CH, P), F32, kind="ExternalOutput").ap()
    build(nc, *args, out)
    r = run_bass_kernel_spmd(nc, [arrays], core_ids=[0])
    out_t = r.results[0]["out_t"].reshape(P, B, CH, P)
    return np.ascontiguousarray(out_t.transpose(1, 3, 2, 0).reshape(B, P, L))
```

```python
from contextlib import ExitStack

import concourse.bass as bass
from concourse import mybir
from concourse.alu_op_type import AluOpType as ALU

F32 = mybir.dt.float32
F32R = mybir.dt.float32r
ACT = mybir.ActivationFunctionType
AX_X = mybir.AxisListType.X

P = 128
B = 8
L = 256
CH = L // P
HEADS = 16
HD = 8
PAIRS = HD * (HD + 1) // 2
E = 16
TOPK = 4
F = 128
WE = 6 * P
GU = 4 * P
GROUPS = [4, 4]
NG = len(GROUPS)
NBM = max(GROUPS)
B0 = [sum(GROUPS[:g]) for g in range(NG)]
STEPS = E + 1
HB = 4
BLOCKS = HEADS // HB
KV0 = 4
BC = HB * HD
LOOP_E = 3
RING = 3
EPS = 1e-5
SENT = -3.0e38
TAKEN = -1.0e38
SCW = E + TOPK
PAIR_AT = [sum(HD - e for e in range(d)) for d in range(HD)]


def build(nc, kpad, dskip, d_rows, ctx_t, x_nat, x_t, w_all, router_t, bias_rows, out_t):
    with ExitStack() as ctx:
        def sb(name, shape, dt=F32):
            return ctx.enter_context(nc.sbuf_tensor(name, shape, dt))

        def sem(name):
            return ctx.enter_context(nc.semaphore(name))

        krow = sb("krow", [HEADS, P + L])
        drow = sb("drow", [HEADS, 1])
        ctxT = sb("ctxT", [P, B * CH, P])
        xnat = sb("xnat", [P, B, L])
        x1T = sb("x1T", [P, B * CH, P])
        toep = sb("toep", [P, HEADS * L])
        toep_w = sb("toep_w", [P, HB, L])
        W = NBM * CH * PAIRS
        ZW = NBM * CH * BC
        kv = sb("kv", [P, 2, HB, W])
        Y = sb("Y", [P, 2, HB, W])
        Z = sb("Z", [P, 2, HD, ZW])
        qT = sb("qT", [P, B * CH, P])
        wraw = sb("wraw", [P, STEPS * WE])
        whi = sb("whi", [P, RING, WE], F32R)
        wlo = sb("wlo", [P, RING, WE], F32R)
        hn = sb("hn", [P, NBM, L])
        NTM = NBM * P
        hhi = sb("hhi", [P, 2, CH, NTM], F32R)
        hlo = sb("hlo", [P, 2, CH, NTM], F32R)
        sg = sb("sg", [P, NTM])
        tw = sb("tw", [P, NTM])
        av = sb("av", [P, RING, NTM])
        ahi = sb("ahi", [P, RING, NTM], F32R)
        alo = sb("alo", [P, RING, NTM], F32R)
        ident = sb("ident", [P, P])
        selcol = sb("selcol", [P, E])
        sel = sb("sel", [P, RING, P], F32R)
        rraw = sb("rraw", [P, CH * E])
        rhi = sb("rhi", [P, CH * E], F32R)
        rlo = sb("rlo", [P, CH * E], F32R)
        bias = sb("bias", [P, E])
        stats = sb("stats", [P, NBM, 6])
        mv = sb("mv", [P, 2 * B, 2])
        veps = sb("veps", [P, 2 * B])
        mhalf = sb("mhalf", [P, B])
        rstd = sb("rstd", [P, 2 * B])
        nbias = sb("nbias", [P, 2 * B])
        score = sb("score", [P, NBM, E])
        choice = sb("choice", [P, NBM, SCW])
        left = sb("left", [P, NBM, SCW])
        top = sb("top", [P, NBM, 8])
        chosen = sb("chosen", [P, NBM, E])
        wts = sb("wts", [P, NBM, E])
        tot = sb("tot", [P, NBM])
        tinv = sb("tinv", [P, NBM])
        comb = sb("comb", [P, NBM, P], F32R)
        combT = sb("combT", [P, NTM], F32R)
        flip = sb("flip", [P, P])
        dcol = sb("dcol", [P, HEADS])

        acc = [ctx.enter_context(nc.psum_tensor(f"acc{c}", [P, 512], F32)) for c in range(CH)]
        G = ctx.enter_context(nc.psum_tensor("G", [P, 512], F32))
        U = ctx.enter_context(nc.psum_tensor("U", [P, 512], F32))
        CB = ctx.enter_context(nc.psum_tensor("CB", [P, 512], F32))
        C = [ctx.enter_context(nc.psum_tensor(f"C{i}", [P, 512], F32)) for i in range(3)]

        toep_dram = nc.dram_tensor("toep_rows", (HEADS, P + L), F32, kind="Internal")

        s_k = sem("kernel_rows_loaded")
        s_kd = sem("kernel_rows_with_d")
        s_kout = sem("kernel_rows_stored")
        s_toep0 = sem("toeplitz_block0_loaded")
        s_toep = sem("toeplitz_rest_loaded")
        s_tdiag = sem("toeplitz_block0_with_d")
        s_ctx = [sem(f"ctx_loaded{g}") for g in range(NG)]
        s_x = [sem(f"x_loaded{g}") for g in range(NG)]
        s_xT = [sem(f"xT_loaded{g}") for g in range(NG)]
        s_dcol = sem("d_loaded")
        s_router = sem("router_loaded")
        s_bias = sem("bias_loaded")
        s_w = [sem(f"weights_loaded{i}") for i in range(3)]
        s_const = sem("constants_ready")
        s_cstep = sem("constants_step")
        s_chain = sem("vector_chain")
        s_rhi = sem("router_hi")
        s_rlo = sem("router_lo")
        s_var = sem("variances_ready")
        s_rstd = sem("rstd_ready")
        s_nb = sem("norm_bias_ready")
        s_norm = sem("rows_normalised")
        s_qtp = sem("queries_transposed")
        s_q = sem("queries_ready")
        s_kv0 = sem("kv_block0_vector_part")
        s_kv = sem("kv_ready")
        s_tw = sem("block_toeplitz_ready")
        s_conv = sem("heads_convolved")
        s_y = sem("heads_evacuated")
        s_terms = sem("terms_formed")
        s_zp = sem("pool_terms_added")
        s_sum = sem("terms_sum_step")
        s_x1 = sem("attention_added")
        s_xn = sem("x1_transposed")
        s_htp = sem("h_transposed")
        s_hh = sem("h_hi")
        s_hl = sem("h_lo")
        s_lg = sem("logits_ready")
        s_sc = sem("scores_ready")
        s_cx = sem("combine_ready")
        s_ctp = sem("combine_transposed")
        s_comb = sem("combine_in_place")
        s_wgh = sem("gate_up_hi")
        s_wgl = sem("gate_up_lo")
        s_wdh = sem("down_hi")
        s_wdl = sem("down_lo")
        s_sel = sem("select_ready")
        s_spr = sem("combine_spread")
        s_g = sem("gate_ready")
        s_u = sem("up_ready")
        s_silu = sem("silu_ready")
        s_t = sem("weighted_silu_ready")
        s_a = sem("act_ready")
        s_ah = sem("act_hi")
        s_al = sem("act_lo")
        s_acc = sem("group_accumulated")
        s_res = sem("result_ready")
        s_out = sem("result_stored")

        kdram = toep_dram.ap()
        block = ctx.enter_context(nc.Block())

        def gsl(g):
            return slice(B0[g] * CH, (B0[g] + GROUPS[g]) * CH)

        def lncols(i):
            return (4 * i, NBM) if i < 2 else (6 + i, 1) if i < 6 else (12, NBM)

        def wcols(s, first, n):
            return wraw[:, bass.ds(s * WE + first, n)]

        def toeplitz_rows(rows, h0, h1):
            return bass.AP(rows.tensor, rows.offset + h0 * (P + L) + 1, [[1, P], [P + L, h1 - h0], [1, L]])

        toep_h = toep[:, :].rearrange("p (h l) -> p h l", h=HEADS)

        def conv_bank(h):
            return (C[0], C[1], C[2], CB)[h]

        def xn_bank(k):
            return (G, U)[k % 2]

        def x1_row(b):
            return C[b // 2][:, (b % 2) * L:(b % 2 + 1) * L]

        x1_first = x1T[:, gsl(0), :].rearrange("p (k c) n -> p k c n", c=CH)

        @block.sync
        def _(sp):
            sp.dma_start(toep_h[:, 0:HB, :], toeplitz_rows(kpad, 0, HB)).then_inc(s_toep0, 16)
            sp.dma_start(xnat[:, 0:NBM, :], x_nat[0:NBM].rearrange("b p l -> p b l")).then_inc(s_x[0], 16)
            sp.wait_ge(s_kd, 1)
            sp.dma_start(kdram, krow[:, :]).then_inc(s_kout, 16)
            sp.dma_start(x1T[:, gsl(0), :], x_t[:, gsl(0), :]).then_inc(s_xT[0], 16)
            sp.wait_ge(s_kout, 16)
            sp.dma_start(toep_h[:, HB:HEADS, :], toeplitz_rows(kdram, HB, HEADS)).then_inc(s_toep, 16)
            for i, (a, b) in enumerate(((0, 1), (1, 3), (3, STEPS))):
                sp.dma_start(wraw[:, a * WE:b * WE], w_all[:, a * WE:b * WE]).then_inc(s_w[i], 16)
            sp.dma_start(x1T[:, gsl(1), :], x_t[:, gsl(1), :]).then_inc(s_xT[1], 16)
            for g in range(NG):
                sp.wait_ge(s_res, g + 1)
                sp.dma_start(out_t[:, gsl(g), :], x1T[:, gsl(g), :]).then_inc(s_out, 16)
            sp.wait_ge(s_out, 16 * NG)

        @block.gpsimd
        def _(pool):
            tt = nc.gpsimd.tensor_tensor

            def rsqrt(i):
                pool.wait_ge(s_var, i + 1)
                c, n = lncols(i)
                tt(rstd[:, c:c + n], veps[:, c:c + n], mhalf[:, 0:n], ALU.pow).then_inc(s_rstd, 1)

            def kv_block(g, k, buf, first=0):
                x = ctxT[:, gsl(g), bass.ds(k * BC, BC)].rearrange("p c (h i) -> p h c i", i=HD)
                dst = kv[:, buf, :, :].rearrange("p h (c n) -> p h c n", n=PAIRS)
                for d in range(first, HD):
                    ins = tt(dst[:, :, :, PAIR_AT[d]:PAIR_AT[d] + HD - d], x[:, :, :, 0:HD - d],
                             x[:, :, :, d:HD], ALU.mult)
                ins.then_inc(s_kv, 1)

            def add_half(k):
                pool.wait_ge(s_terms, k + 1)
                z = Z[:, k % 2]
                tt(z[:, 0:2, :], z[:, 0:2, :], z[:, 4:6, :], ALU.add).then_inc(s_zp, 1)

            def gate_up_lo(n, r, s):
                pool.wait_ge(s_wgh, n + 1)
                tt(wlo[:, r, 0:GU], wcols(s, 0, GU), whi[:, r, 0:GU].bitcast(F32), ALU.subtract).then_inc(s_wgl, 1)

            def act_lo(g, n, r):
                pool.wait_ge(s_ah, n + 1)
                nt = GROUPS[g] * P
                tt(alo[:, r, 0:nt], av[:, r, 0:nt], ahi[:, r, 0:nt].bitcast(F32), ALU.subtract).then_inc(s_al, 1)

            nc.gpsimd.memset(mhalf[:, :], -0.5).then_inc(s_cstep, 1)
            nc.gpsimd.memset(ident[:, :], 0.0).then_inc(s_cstep, 1)
            nc.gpsimd.memset(selcol[:, :], 0.0).then_inc(s_cstep, 1)
            nc.gpsimd.memset(flip[:, :], 0.0).then_inc(s_cstep, 1)
            pool.wait_ge(s_cstep, 4)
            nc.gpsimd.affine_select(out=flip[:, :], in_=flip[:, :], compare_op=ALU.not_equal, fill=1.0,
                                    base=1 - P, pattern=[[1, P]], channel_multiplier=1).then_inc(s_const, 1)
            nc.gpsimd.affine_select(out=ident[:, :], in_=ident[:, :], compare_op=ALU.not_equal, fill=1.0,
                                    base=0, pattern=[[-1, P]], channel_multiplier=1).then_inc(s_const, 1)
            nc.gpsimd.affine_select(out=selcol[:, :], in_=selcol[:, :], compare_op=ALU.not_equal, fill=1.0,
                                    base=0, pattern=[[-1, E]], channel_multiplier=1).then_inc(s_cstep, 1)
            pool.wait_ge(s_cstep, 5)
            nc.gpsimd.affine_select(out=selcol[:, :], in_=selcol[:, :], compare_op=ALU.not_equal, fill=1.0,
                                    base=-E, pattern=[[-1, E]], channel_multiplier=1).then_inc(s_const, 1)
            pool.wait_ge(s_ctx[0], 16)
            kv_block(0, 0, 0, KV0)
            rsqrt(0)
            kv_block(0, 1, 1)
            rsqrt(1)
            for k in range(2, BLOCKS):
                add_half(k - 2)
                pool.wait_ge(s_conv, HB * (k - 1))
                kv_block(0, k, k % 2)
                if k == 3:
                    rsqrt(2)
            add_half(2)
            rsqrt(3)
            add_half(3)
            rsqrt(4)
            for m in range(2):
                gate_up_lo(m, m, m)
            rsqrt(5)
            for g in range(NG):
                n0 = g * STEPS
                nxt = g + 1 < NG
                gate_up_lo(n0 + 2, (n0 + 2) % RING, 2)
                if nxt:
                    pool.wait_ge(s_ctx[g + 1], 16)
                    kv_block(g + 1, 0, 0)
                act_lo(g, n0, n0 % RING)
                with pool.Fori(0, BLOCKS - 1) as k:
                    for j in range(LOOP_E):
                        n = n0 + 1 + j
                        gate_up_lo(k * LOOP_E + (n + 2), (n + 2) % RING, k * LOOP_E + (3 + j))
                        act_lo(g, k * LOOP_E + n, n % RING)
                        if nxt and j == 0:
                            pool.wait_ge(s_conv, k * HB + HB * (BLOCKS + 1))
                            kv_block(g + 1, k + 1, 0)
                for s in range(1 + LOOP_E * (BLOCKS - 1), STEPS):
                    n = n0 + s
                    if s + 2 < STEPS or nxt:
                        gate_up_lo(n + 2, (n + 2) % RING, (s + 2) % STEPS)
                    act_lo(g, n, n % RING)
                    if nxt and s == 13:
                        rsqrt(6)

        @block.scalar
        def _(act):
            def normalise(i, dst, src):
                act.wait_ge(s_nb, i + 1)
                c, n = lncols(i)
                for b in range(n):
                    ins = nc.scalar.activation(dst(b), src(b), ACT.Identity, bias=nbias[:, c + b:c + b + 1],
                                               scale=rstd[:, c + b:c + b + 1])
                ins.then_inc(s_norm, 1)

            def query_rows(g):
                act.wait_ge(s_x[g], 16)
                normalise(g, lambda b: hn[:, b, :], lambda b: xnat[:, B0[g] + b, :])

            def queries(g):
                act.wait_ge(s_qtp, g + 1)
                dst = qT[:, gsl(g), :].rearrange("p (a c) n -> p a (c n)", a=2)
                for a in range(2):
                    ins = nc.scalar.copy(dst[:, a, :], acc[a][:, :])
                ins.then_inc(s_q, 1)

            def evacuate(g, k, buf, bank):
                for h in range(HB):
                    act.wait_ge(s_conv, k * HB + (HB * BLOCKS * g + h + 1))
                    nc.scalar.copy(Y[:, buf, h, :], bank(h)[:, 0:W]).then_inc(s_y, 1)

            def gate_up_hi(r, s):
                nc.scalar.copy(whi[:, r, 0:GU], wcols(s, 0, GU)).then_inc(s_wgh, 1)

            def down_hi(r, s):
                nc.scalar.copy(whi[:, r, GU:WE], wcols(s, GU, WE - GU)).then_inc(s_wdh, 1)

            def silu(g, n):
                act.wait_ge(s_g, n + 1)
                nt = GROUPS[g] * P
                nc.scalar.activation(sg[:, 0:nt], G[:, 0:nt], ACT.Silu).then_inc(s_silu, 1)

            def act_hi(g, n, r):
                act.wait_ge(s_a, n + 1)
                nt = GROUPS[g] * P
                nc.scalar.copy(ahi[:, r, 0:nt], av[:, r, 0:nt]).then_inc(s_ah, 1)

            def h_hi_block(k):
                act.wait_ge(s_htp, k + 1)
                nc.scalar.copy(hhi[:, 0, :, k * P:(k + 1) * P],
                               acc[k % 2][:, 0:L].rearrange("p (c n) -> p c n", c=CH)).then_inc(s_hh, 1)

            def scores(g, bank):
                act.wait_ge(s_lg, g + 1)
                nc.scalar.activation(score[:, :, :].rearrange("p b e -> p (b e)"), bank[:, 0:NBM * E],
                                     ACT.Sigmoid).then_inc(s_sc, 1)

            def combine_in_place(g):
                act.wait_ge(s_ctp, g + 1)
                nc.scalar.copy(combT[:, :], C[2][:, :]).then_inc(s_comb, 1)

            act.dma_start(krow[:, :], kpad).then_inc(s_k, 16)
            act.dma_start(drow[:, :], dskip).then_inc(s_k, 16)
            act.dma_start(dcol[:, :], d_rows).then_inc(s_dcol, 16)
            act.dma_start(ctxT[:, gsl(0), :], ctx_t[:, gsl(0), :]).then_inc(s_ctx[0], 16)
            act.dma_start(rraw[:, :], router_t).then_inc(s_router, 16)
            act.dma_start(bias[:, :], bias_rows).then_inc(s_bias, 16)
            act.dma_start(xnat[:, NBM:B, :], x_nat[NBM:B].rearrange("b p l -> p b l")).then_inc(s_x[1], 16)
            act.dma_start(ctxT[:, gsl(1), :], ctx_t[:, gsl(1), :]).then_inc(s_ctx[1], 16)
            act.wait_ge(s_router, 16)
            nc.scalar.copy(rhi[:, :], rraw[:, :]).then_inc(s_rhi, 1)
            query_rows(0)
            queries(0)
            evacuate(0, 0, 0, conv_bank)
            query_rows(1)
            queries(1)
            evacuate(0, 1, 1, conv_bank)
            for k in range(BLOCKS):
                if k + 2 < BLOCKS:
                    normalise(2 + k, lambda b: hn[:, 0, :], lambda b, k=k: xn_bank(k)[:, 0:L])
                    act.wait_ge(s_terms, k + 1)
                    evacuate(0, k + 2, k % 2, conv_bank)
                    h_hi_block(k)
                else:
                    normalise(2 + k, lambda b: hn[:, 0, :], lambda b, k=k: xn_bank(k)[:, 0:L])
                    if k == 2:
                        act.wait_ge(s_w[0], 16)
                        gate_up_hi(0, 0)
                        down_hi(0, 0)
                    h_hi_block(k)
                    if k == 2:
                        act.wait_ge(s_w[1], 16)
                        gate_up_hi(1, 1)
            scores(0, C[0])
            for g in range(NG):
                n0 = g * STEPS
                nxt = g + 1 < NG
                silu(g, n0)
                gate_up_hi((n0 + 2) % RING, 2)
                down_hi((n0 + 1) % RING, 1)
                act_hi(g, n0, n0 % RING)
                combine_in_place(g)
                if g == 0:
                    act.wait_ge(s_w[2], 16)
                    act.wait_ge(s_toep, 16)
                with act.Fori(0, BLOCKS) as k:
                    if nxt:
                        nc.scalar.copy(toep_w[:, :, :].rearrange("p h l -> p (h l)"),
                                       toep[:, bass.ds(k * HB * L, HB * L)]).then_inc(s_tw, 1)
                    for j in range(LOOP_E):
                        n = n0 + 1 + j
                        silu(g, k * LOOP_E + n)
                        gate_up_hi((n + 2) % RING, k * LOOP_E + (3 + j))
                        down_hi((n + 1) % RING, k * LOOP_E + (2 + j))
                        act_hi(g, k * LOOP_E + n, n % RING)
                        if nxt and j == 0:
                            act.wait_ge(s_terms, k + BLOCKS * (g + 1))
                            evacuate(g + 1, k, 0, lambda h: C[h % 3])
                for s in range(1 + LOOP_E * BLOCKS, STEPS):
                    n = n0 + s
                    silu(g, n)
                    if s + 2 < STEPS or nxt:
                        gate_up_hi((n + 2) % RING, (s + 2) % STEPS)
                    if s + 1 < STEPS or nxt:
                        down_hi((n + 1) % RING, (s + 1) % STEPS)
                    act_hi(g, n, n % RING)
                    if nxt and s == 14:
                        normalise(6, lambda b: hn[:, b, :], x1_row)
                    if nxt and s == 15:
                        act.wait_ge(s_htp, BLOCKS + 1)
                        nc.scalar.copy(hhi[:, 1, 0, :], C[2][:, :]).then_inc(s_hh, 1)
                        nc.scalar.copy(hhi[:, 1, 1, :], C[0][:, :]).then_inc(s_hh, 1)
                if nxt:
                    scores(g + 1, C[1])

        @block.vector
        def _(dve):
            tt = nc.vector.tensor_tensor
            chain = [0]

            def link(ins):
                chain[0] += 1
                ins.then_inc(s_chain, 1)
                dve.wait_ge(s_chain, chain[0])

            def statistics(i, rows):
                c, n = lncols(i)
                for b in range(n):
                    ins = nc.vector.bn_stats(stats[:, b, :], rows(b))
                link(ins)
                for b in range(n):
                    ins = nc.vector.bn_aggr(mv[:, c + b, :], stats[:, b, :])
                link(ins)
                nc.vector.tensor_scalar(veps[:, c:c + n], mv[:, c:c + n, 1], EPS, None,
                                        ALU.add).then_inc(s_var, 1)

            def norm_bias(i):
                dve.wait_ge(s_rstd, i + 1)
                c, n = lncols(i)
                nc.vector.scalar_tensor_tensor(out=nbias[:, c:c + n], in0=mv[:, c:c + n, 0], scalar=-1.0,
                                               in1=rstd[:, c:c + n], op0=ALU.mult, op1=ALU.mult).then_inc(s_nb, 1)

            TERMS = [(d, d, 0, d) for d in range(HD)] + [(d, HD - d, d, 0) for d in range(1, HD)]

            def terms(g, k, buf, first, last):
                y = Y[:, buf].rearrange("p h (c n) -> p h c n", n=PAIRS)
                q = qT[:, gsl(g), bass.ds(k * BC, BC)].rearrange("p c (h i) -> p h c i", i=HD)
                z = Z[:, buf].rearrange("p e (c h j) -> p e h c j", h=HB, j=HD)
                for d, e, qi, zj in TERMS[first:last]:
                    ins = tt(z[:, e, :, :, zj:zj + HD - d], y[:, :, :, PAIR_AT[d]:PAIR_AT[d] + HD - d],
                             q[:, :, :, qi:qi + HD - d], ALU.mult)
                return ins

            def add_to_x(g, k, buf):
                z = Z[:, buf, 0, :].rearrange("p (b c n) -> p b c n", c=CH, n=BC)
                if g == 0:
                    x = x1_first[:, k].rearrange("p c (b n) -> p c b n", n=BC)
                    z = z.rearrange("p b c n -> p c b n")
                else:
                    x = x1T[:, gsl(g), bass.ds(k * BC, BC)].rearrange("p (b c) n -> p b c n", c=CH)
                tt(x, x, z, ALU.add).then_inc(s_x1, 1)

            def first_terms(k):
                dve.wait_ge(s_y, HB * (k + 1))
                if k >= 2:
                    dve.wait_ge(s_x1, k - 1)
                terms(0, k, k % 2, 0, len(TERMS)).then_inc(s_terms, 1)

            def first_sums(k):
                z = Z[:, k % 2]
                dve.wait_ge(s_terms, k + 1)
                link(tt(z[:, 2:4, :], z[:, 2:4, :], z[:, 6:8, :], ALU.add))
                dve.wait_ge(s_zp, k + 1)
                link(tt(z[:, 0:2, :], z[:, 0:2, :], z[:, 2:4, :], ALU.add))
                link(tt(z[:, 0, :], z[:, 0, :], z[:, 1, :], ALU.add))
                add_to_x(0, k, k % 2)

            def next_terms(g, k, first, last):
                return terms(g, k, 0, first, last)

            def next_sums(g, k):
                z = Z[:, 0]
                for i, half in enumerate((4, 2, 1)):
                    if i == 0:
                        dve.wait_ge(s_terms, k + (BLOCKS * g + 1))
                    else:
                        dve.wait_ge(s_sum, 3 * k + (3 * BLOCKS * (g - 1) + i))
                    tt(z[:, 0:half, :], z[:, 0:half, :], z[:, half:2 * half, :], ALU.add).then_inc(s_sum, 1)
                dve.wait_ge(s_sum, 3 * k + (3 * BLOCKS * (g - 1) + 3))
                add_to_x(g, k, 0)

            def select(r, s):
                nc.vector.tensor_copy(sel[:, r, :], selcol[:, bass.ds(s - 1, 1)].to_broadcast([P, P])).then_inc(s_sel, 1)

            def down_lo(n, r, s):
                dve.wait_ge(s_wdh, n + 1)
                tt(wlo[:, r, GU:WE], wcols(s, GU, WE - GU), whi[:, r, GU:WE].bitcast(F32),
                   ALU.subtract).then_inc(s_wdl, 1)

            def activations(g, n, r, at):
                nt = GROUPS[g] * P
                dve.wait_ge(s_silu, n + 1)
                gate = sg
                if at is not None:
                    dve.wait_ge(s_spr, at + 1)
                    tt(tw[:, 0:nt], sg[:, 0:nt], CB[:, 0:nt], ALU.mult).then_inc(s_t, 1)
                    dve.wait_ge(s_t, at + 1)
                    gate = tw
                dve.wait_ge(s_u, n + 1)
                tt(av[:, r, 0:nt], gate[:, 0:nt], U[:, 0:nt], ALU.mult).then_inc(s_a, 1)

            def h_lo_block(k):
                dve.wait_ge(s_hh, k + 1)
                tt(hlo[:, 0, :, k * P:(k + 1) * P], acc[k % 2][:, 0:L].rearrange("p (c n) -> p c n", c=CH),
                   hhi[:, 0, :, k * P:(k + 1) * P].bitcast(F32), ALU.subtract).then_inc(s_hl, 1)

            def combine(g):
                n = GROUPS[g]
                dve.wait_ge(s_sc, g + 1)
                link(tt(choice[:, 0:n, 0:E], score[:, 0:n, :],
                        bias[:, :].unsqueeze(1).to_broadcast([P, n, E]), ALU.add))
                for b in range(n):
                    ins = nc.vector.max(top[:, b, :], choice[:, b, 0:E])
                link(ins)
                link(nc.vector.memset(top[:, 0:n, TOPK:8], SENT))
                for b in range(n):
                    ins = nc.vector.match_replace(out=left[:, b, :], in_to_replace=top[:, b, :],
                                                  in_values=choice[:, b, :], imm_value=TAKEN)
                link(ins)
                link(tt(chosen[:, 0:n, :], choice[:, 0:n, 0:E], left[:, 0:n, 0:E], ALU.not_equal))
                link(tt(wts[:, 0:n, :], score[:, 0:n, :], chosen[:, 0:n, :], ALU.mult))
                link(nc.vector.tensor_reduce(tot[:, 0:n], wts[:, 0:n, :], AX_X, ALU.add))
                link(nc.vector.tensor_scalar(tot[:, 0:n], tot[:, 0:n], 1e-20, None, ALU.add))
                link(nc.vector.reciprocal(tinv[:, 0:n], tot[:, 0:n]))
                link(tt(wts[:, 0:n, :], wts[:, 0:n, :], tinv[:, 0:n].unsqueeze(2).to_broadcast([P, n, E]), ALU.mult))
                link(nc.vector.tensor_copy(comb[:, 0:n, 0:E], wts[:, 0:n, :]))
                tt(comb[:, 0:n, E:2 * E], wts[:, 0:n, :], comb[:, 0:n, 0:E].bitcast(F32),
                   ALU.subtract).then_inc(s_cx, 1)

            def result(g):
                dve.wait_ge(s_acc, g + 1)
                for c in range(CH):
                    if g == 0:
                        x = x1_first[:, :, c, :]
                        y = acc[c][:, :].rearrange("p (k n) -> p k n", k=BLOCKS)
                    else:
                        x = x1T[:, gsl(g), :].rearrange("p (b c) n -> p c b n", c=CH)[:, c]
                        y = acc[c][:, :].rearrange("p (b n) -> p b n", n=P)
                    ins = tt(x, y, x, ALU.add)
                ins.then_inc(s_res, 1)

            dve.wait_ge(s_k, 32)
            tt(krow[:, P:P + 1], krow[:, P:P + 1], drow[:, :], ALU.add).then_inc(s_kd, 1)
            dve.wait_ge(s_ctx[0], 16)
            x = ctxT[:, gsl(0), 0:BC].rearrange("p c (h i) -> p h c i", i=HD)
            dst = kv[:, 0, :, :].rearrange("p h (c n) -> p h c n", n=PAIRS)
            for d in range(KV0):
                ins = tt(dst[:, :, :, PAIR_AT[d]:PAIR_AT[d] + HD - d], x[:, :, :, 0:HD - d], x[:, :, :, d:HD], ALU.mult)
            ins.then_inc(s_kv0, 1)
            dve.wait_ge(s_toep0, 16)
            dve.wait_ge(s_dcol, 16)
            dve.wait_ge(s_const, 1)
            for h in range(HB):
                ins = nc.vector.scalar_tensor_tensor(out=toep_h[:, h, 0:P], in0=flip[:, :], scalar=dcol[:, h:h + 1],
                                                     in1=toep_h[:, h, 0:P], op0=ALU.mult, op1=ALU.add)
            ins.then_inc(s_tdiag, 1)
            dve.wait_ge(s_x[0], 16)
            statistics(0, lambda b: xnat[:, b, :])
            link(nc.vector.memset(comb[:, :, :].bitcast(F32), 0.0))
            link(nc.vector.memset(choice[:, :, :], SENT))
            norm_bias(0)
            dve.wait_ge(s_rhi, 1)
            tt(rlo[:, :], rraw[:, :], rhi[:, :].bitcast(F32), ALU.subtract).then_inc(s_rlo, 1)
            dve.wait_ge(s_x[1], 16)
            statistics(1, lambda b: xnat[:, NBM + b, :])
            norm_bias(1)
            dve.wait_ge(s_q, 1)
            dve.wait_ge(s_xT[0], 16)
            for k in range(BLOCKS + 1):
                if k < BLOCKS:
                    first_terms(k)
                if k >= 1:
                    dve.wait_ge(s_xn, k)
                    statistics(2 + k - 1, lambda b, k=k: xn_bank(k - 1)[:, 0:L])
                if 2 <= k:
                    h_lo_block(k - 2)
                if k < BLOCKS:
                    first_sums(k)
                if k >= 1:
                    norm_bias(2 + k - 1)
            dve.wait_ge(s_w[0], 16)
            down_lo(0, 0, 0)
            h_lo_block(BLOCKS - 1)
            dve.wait_ge(s_bias, 16)
            dve.wait_ge(s_const, 3)
            combine(0)
            for g in range(NG):
                n0 = g * STEPS
                nxt = g + 1 < NG
                activations(g, n0, n0 % RING, None)
                select((n0 + 1) % RING, 1)
                down_lo(n0 + 1, (n0 + 1) % RING, 1)
                if g:
                    result(g - 1)
                if nxt:
                    dve.wait_ge(s_q, g + 2)
                    dve.wait_ge(s_xT[g + 1], 16)
                with dve.Fori(0, BLOCKS) as k:
                    for j in range(LOOP_E):
                        n = n0 + 1 + j
                        activations(g, k * LOOP_E + n, n % RING, k * LOOP_E + (g * E + j))
                        select((n + 1) % RING, k * LOOP_E + (2 + j))
                        down_lo(k * LOOP_E + (n + 1), (n + 1) % RING, k * LOOP_E + (2 + j))
                        if nxt and j == 1:
                            dve.wait_ge(s_y, k * HB + (HB * BLOCKS * (g + 1) + HB))
                            dve.wait_ge(s_x1, k + BLOCKS * (g + 1))
                            next_terms(g + 1, k, 0, 7)
                        if nxt and j == 2:
                            next_terms(g + 1, k, 7, len(TERMS)).then_inc(s_terms, 1)
                            next_sums(g + 1, k)
                for s in range(1 + LOOP_E * BLOCKS, STEPS):
                    n = n0 + s
                    activations(g, n, n % RING, g * E + s - 1)
                    if s + 1 < STEPS:
                        select((n + 1) % RING, s + 1)
                    if s + 1 < STEPS or nxt:
                        down_lo(n + 1, (n + 1) % RING, (s + 1) % STEPS)
                    if nxt and s == 13:
                        dve.wait_ge(s_xn, BLOCKS + 1)
                        statistics(6, x1_row)
                    if nxt and s == 14:
                        norm_bias(6)
                    if nxt and s == 15:
                        for c, src in enumerate((C[2], C[0])):
                            dve.wait_ge(s_hh, BLOCKS + c + 1)
                            ins = tt(hlo[:, 1, c, :], src[:, :], hhi[:, 1, c, :].bitcast(F32), ALU.subtract)
                        ins.then_inc(s_hl, 1)
                if nxt:
                    combine(g + 1)
            result(NG - 1)

        @block.tensor
        def _(pe):
            mm = nc.tensor.matmul

            def queries(g):
                pe.wait_ge(s_norm, g + 1)
                if g:
                    pe.wait_ge(s_q, g)
                for b in range(GROUPS[g]):
                    for c in range(CH):
                        at = (b % 2) * L + c * P
                        ins = nc.tensor.transpose(acc[b // 2][:, at:at + P], hn[:, b, c * P:(c + 1) * P], ident[:, :])
                ins.then_inc(s_qtp, 1)

            def convolve(g, h, buf, out, matrices):
                m = kv[:, buf, h, :].rearrange("p (b c n) -> p b c n", c=CH, n=PAIRS)
                y = out[:, 0:W].rearrange("p (b c n) -> p b c n", c=CH, n=PAIRS)
                near, far = matrices[:, 0:P], matrices[:, P:L]
                mm(y[:, :, 0, :], near, m[:, :, 0, :], start=True, stop=True)
                mm(y[:, :, 1, :], near, m[:, :, 1, :], start=True, stop=False)
                mm(y[:, :, 1, :], far, m[:, :, 0, :], start=False, stop=True).then_inc(s_conv, 1)

            def convolve_first(k):
                pe.wait_ge(s_kv, k + 1)
                for h in range(HB):
                    if k:
                        pe.wait_ge(s_y, HB * (k - 1) + h + 1)
                    convolve(0, h, k % 2, conv_bank(h), toep_h[:, HB * k + h, :])

            def x1_rows_block(k):
                pe.wait_ge(s_x1, k + 1)
                for c in range(CH):
                    ins = nc.tensor.transpose(xn_bank(k)[:, c * P:(c + 1) * P], x1_first[:, k, c, :], ident[:, :])
                ins.then_inc(s_xn, 1)

            def h_block(k):
                pe.wait_ge(s_norm, 2 + k + 1)
                if k == 0:
                    pe.wait_ge(s_q, NG)
                if k >= 2:
                    pe.wait_ge(s_hl, k - 1)
                for c in range(CH):
                    ins = nc.tensor.transpose(acc[k % 2][:, c * P:(c + 1) * P], hn[:, 0, c * P:(c + 1) * P],
                                              ident[:, :])
                ins.then_inc(s_htp, 1)

            def product3(out, whi_, wlo_, xhi, xlo, start, stop):
                mm(out, whi_, xhi, start=start, stop=False, skip_group_check=True)
                mm(out, whi_, xlo, start=False, stop=False, skip_group_check=True)
                return mm(out, wlo_, xhi, start=False, stop=stop, skip_group_check=True)

            def router(g, b, bank):
                out = bank[:, b * E:(b + 1) * E]
                for c in range(CH):
                    h1, h2 = (t[:, g % 2, c, b * P:(b + 1) * P] for t in (hhi, hlo))
                    r1, r2 = (t[:, c * E:(c + 1) * E] for t in (rhi, rlo))
                    mm(out, h1, r1, start=(c == 0), stop=False)
                    mm(out, h1, r2, start=False, stop=False)
                    ins = mm(out, h2, r1, start=False, stop=(c == CH - 1))
                return ins

            def combine_turned(g):
                pe.wait_ge(s_cx, g + 1)
                for b in range(GROUPS[g]):
                    ins = nc.tensor.transpose(C[2][:, b * P:(b + 1) * P], comb[:, b, :].bitcast(F32), ident[:, :])
                ins.then_inc(s_ctp, 1)
                pe.wait_ge(s_comb, g + 1)

            def spread(g, n, r, s):
                pe.wait_ge(s_a, n)
                pe.wait_ge(s_sel, g * E + s)
                mm(CB[:, 0:GROUPS[g] * P], sel[:, r, :], combT[:, 0:GROUPS[g] * P], start=True,
                   stop=True).then_inc(s_spr, 1)

            def hidden(g, r, half, out, done):
                nt = GROUPS[g] * P
                for c in range(CH):
                    at = (2 * half + c) * P
                    ins = product3(out[:, 0:nt], whi[:, r, at:at + P], wlo[:, r, at:at + P],
                                   hhi[:, g % 2, c, 0:nt], hlo[:, g % 2, c, 0:nt], c == 0, c == CH - 1)
                ins.then_inc(done, 1)

            def gate(g, n, r):
                pe.wait_ge(s_wgl, n + 1)
                hidden(g, r, 0, G, s_g)

            def up(g, r):
                hidden(g, r, 1, U, s_u)

            def down(g, n, r, first=False, last=False):
                nt = GROUPS[g] * P
                pe.wait_ge(s_al, n + 1)
                pe.wait_ge(s_wdl, n + 1)
                for c in range(CH):
                    at = GU + c * P
                    ins = product3(acc[c][:, 0:nt], whi[:, r, at:at + P], wlo[:, r, at:at + P],
                                   ahi[:, r, 0:nt], alo[:, r, 0:nt], first, last)
                if last:
                    ins.then_inc(s_acc, 1)

            def routed(g, n, n_at, s):
                pe.wait_ge(s_silu, n)
                gate(g, n, n_at % RING)
                spread(g, n, n_at % RING, s)
                up(g, n_at % RING)

            pe.wait_ge(s_const, 3)
            pe.wait_ge(s_kv0, 1)
            pe.wait_ge(s_tdiag, 1)
            convolve_first(0)
            queries(0)
            pe.wait_ge(s_toep, 16)
            convolve_first(1)
            queries(1)
            x1_rows_block(0)
            convolve_first(2)
            h_block(0)
            x1_rows_block(1)
            convolve_first(3)
            h_block(1)
            pe.wait_ge(s_rlo, 1)
            pe.wait_ge(s_y, HB * BLOCKS)
            x1_rows_block(2)
            for b in range(BLOCKS):
                if b + 2 < BLOCKS:
                    h_block(b + 2)
                    if b + 3 < BLOCKS:
                        x1_rows_block(b + 3)
                pe.wait_ge(s_hl, b + 1)
                ins = router(0, b, C[0])
            ins.then_inc(s_lg, 1)
            for g in range(NG):
                n0 = g * STEPS
                nxt = g + 1 < NG
                if g:
                    pe.wait_ge(s_silu, n0)
                gate(g, n0, n0 % RING)
                if g:
                    pe.wait_ge(s_a, n0)
                up(g, n0 % RING)
                if g:
                    down(g - 1, n0 - 1, (n0 - 1) % RING, last=True)
                pe.wait_ge(s_silu, n0 + 1)
                gate(g, n0 + 1, (n0 + 1) % RING)
                combine_turned(g)
                spread(g, n0 + 1, (n0 + 1) % RING, 1)
                up(g, (n0 + 1) % RING)
                if g:
                    pe.wait_ge(s_res, g)
                down(g, n0, n0 % RING, first=True)
                with pe.Fori(0, BLOCKS) as k:
                    if nxt:
                        pe.wait_ge(s_kv, k + (BLOCKS * (g + 1) + 1))
                        pe.wait_ge(s_tw, k + (BLOCKS * g + 1))
                        for h in range(HB):
                            if h == 3:
                                pe.wait_ge(s_y, k * HB + (HB * BLOCKS * (g + 1) + 1))
                            convolve(g + 1, h, 0, C[h % 3], toep_w[:, h, :])
                    for j in range(LOOP_E):
                        n = n0 + 2 + j
                        routed(g, k * LOOP_E + n, n, k * LOOP_E + (2 + j))
                        down(g, k * LOOP_E + (n - 1), (n - 1) % RING)
                if nxt:
                    pe.wait_ge(s_x1, BLOCKS * (g + 2))
                    for b in range(NBM):
                        for c in range(CH):
                            ins = nc.tensor.transpose(x1_row(b)[:, c * P:(c + 1) * P],
                                                      x1T[:, (B0[1] + b) * CH + c, :], ident[:, :])
                    ins.then_inc(s_xn, 1)
                for s in range(2 + LOOP_E * BLOCKS, STEPS):
                    n = n0 + s
                    routed(g, n, n, s)
                    down(g, n - 1, (n - 1) % RING)
                    if nxt and s == 15:
                        pe.wait_ge(s_norm, 7)
                        for c, dst in enumerate((C[2], C[0])):
                            for b in range(NBM):
                                ins = nc.tensor.transpose(dst[:, b * P:(b + 1) * P], hn[:, b, c * P:(c + 1) * P],
                                                          ident[:, :])
                        ins.then_inc(s_htp, 1)
                if nxt:
                    pe.wait_ge(s_hl, BLOCKS + 1)
                    for b in range(NBM):
                        ins = router(g + 1, b, C[1])
                    ins.then_inc(s_lg, 1)
            down(NG - 1, NG * STEPS - 1, (NG * STEPS - 1) % RING, last=True)


def kernel(x, ctx_2048, L0_xattn_ssm_kernel, L0_xattn_D, L0_ffn_router_w, L0_ffn_router_bias,
           L0_ffn_expert_gate_w, L0_ffn_expert_up_w, L0_ffn_expert_down_w, L0_ffn_shared_gate_w,
           L0_ffn_shared_up_w, L0_ffn_shared_down_w):
    import numpy as np
    import concourse.bacc as bacc
    from concourse.bass_utils import run_bass_kernel_spmd

    def positions_first(a):
        return np.ascontiguousarray(np.asarray(a).reshape(B, P, CH, P).transpose(3, 0, 2, 1).reshape(P, B * CH, P))

    def tokens_first(a):
        a = np.asarray(a)
        first = a[:NBM].reshape(NBM, BLOCKS, BC, CH, P).transpose(4, 1, 3, 0, 2).reshape(P, NBM * CH, P)
        second = a[NBM:].reshape(NBM, P, CH, P).transpose(3, 0, 2, 1).reshape(P, NBM * CH, P)
        return np.ascontiguousarray(np.concatenate([first, second], 1))

    def with_shared(shared, experts):
        return np.concatenate([np.asarray(shared)[None], np.asarray(experts)], 0)

    def in_first(w):
        return w.reshape(STEPS, F, CH, P).transpose(3, 0, 2, 1).reshape(P, STEPS, CH * F)

    xs = np.asarray(x)
    gate = in_first(with_shared(L0_ffn_shared_gate_w, L0_ffn_expert_gate_w))
    up = in_first(with_shared(L0_ffn_shared_up_w, L0_ffn_expert_up_w))
    down = with_shared(L0_ffn_shared_down_w, L0_ffn_expert_down_w).transpose(2, 0, 1)
    ker = np.asarray(L0_xattn_ssm_kernel)
    arrays = {
        "kernel_rows": np.ascontiguousarray(np.concatenate([np.zeros((HEADS, P), ker.dtype), ker], 1)),
        "d_skip": np.ascontiguousarray(np.asarray(L0_xattn_D).reshape(HEADS, 1)),
        "d_rows": np.ascontiguousarray(np.broadcast_to(np.asarray(L0_xattn_D), (P, HEADS))),
        "ctx_t": np.ascontiguousarray(positions_first(ctx_2048)[::-1]),
        "x_nat": np.ascontiguousarray(xs),
        "x_t": tokens_first(xs),
        "w_all": np.ascontiguousarray(np.concatenate([gate, up, down], 2).reshape(P, STEPS * WE)),
        "router_t": np.ascontiguousarray(
            np.asarray(L0_ffn_router_w).reshape(E, CH, P).transpose(2, 1, 0).reshape(P, CH * E)),
        "bias_rows": np.ascontiguousarray(np.broadcast_to(np.asarray(L0_ffn_router_bias), (P, E))),
    }
    nc = bacc.Bacc("TRN2", target_bir_lowering=False, num_devices=1)
    args = [nc.dram_tensor(name, a.shape, mybir.dt.from_np(a.dtype), kind="ExternalInput").ap()
            for name, a in arrays.items()]
    out = nc.dram_tensor("out_t", (P, B * CH, P), F32, kind="ExternalOutput").ap()
    build(nc, *args, out)
    r = run_bass_kernel_spmd(nc, [arrays], core_ids=[0])
    got = r.results[0]["out_t"]
    first = got[:, :NBM * CH].reshape(P, BLOCKS, CH, NBM, BC).transpose(3, 1, 4, 2, 0).reshape(NBM, P, L)
    second = got[:, NBM * CH:].reshape(P, NBM, CH, P).transpose(1, 3, 2, 0).reshape(NBM, P, L)
    return np.ascontiguousarray(np.concatenate([first, second], 0))
```

```python
from contextlib import ExitStack

import concourse.bass as bass
from concourse import mybir
from concourse.alu_op_type import AluOpType as ALU

F32 = mybir.dt.float32
F32R = mybir.dt.float32r
ACT = mybir.ActivationFunctionType
AX_X = mybir.AxisListType.X

P = 128
B = 8
L = 256
CH = L // P
HEADS = 16
HD = 8
PAIRS = HD * (HD + 1) // 2
E = 16
TOPK = 4
F = 128
WE = 6 * P
GU = 4 * P
GROUPS = [4, 4]
NG = len(GROUPS)
NBM = max(GROUPS)
B0 = [sum(GROUPS[:g]) for g in range(NG)]
STEPS = E + 1
HB = 4
BLOCKS = HEADS // HB
POOL_TERMS = 3
WARM_UP = 37
KVJ = 2
KV0 = 4
BC = HB * HD
ROWS = (STEPS - 2) // 3
LOOP_E = 3
AFTER = 2 + LOOP_E * BLOCKS
RING = 3
NTM = NBM * P
TOKEN_HALVES = (slice(0, NTM // 2), slice(NTM // 2, NTM))
R_LAST = (NG * STEPS - 1) % RING
EPS = 1e-5
SENT = -3.0e38
TAKEN = -1.0e38
SCW = E + TOPK
PAIR_AT = [sum(HD - e for e in range(d)) for d in range(HD)]


def build(nc, kpad, dskip, d_rows, ctx_t, x_nat, x_t, w_all, router_t, bias_rows, out_t):
    with ExitStack() as ctx:
        def sb(name, shape, dt=F32):
            return ctx.enter_context(nc.sbuf_tensor(name, shape, dt))

        def sem(name):
            return ctx.enter_context(nc.semaphore(name))

        krow = sb("krow", [HEADS, P + L])
        drow = sb("drow", [HEADS, 1])
        ctxT = sb("ctxT", [P, B * CH, P])
        xnat = sb("xnat", [P, B, L])
        x1T = sb("x1T", [P, B * CH, P])
        toep = sb("toep", [P, HEADS * L])
        toep_w = sb("toep_w", [P, HB, L])
        W = NBM * CH * PAIRS
        ZW = NBM * CH * BC
        kv = sb("kv", [P, 2, HB, W])
        Y = sb("Y", [P, 2, HB, W])
        Z = sb("Z", [P, 2, HD, ZW])
        qT = sb("qT", [P, B * CH, P])
        wraw = sb("wraw", [P, STEPS * WE])
        whi = sb("whi", [P, RING, WE], F32R)
        wlo = sb("wlo", [P, RING, WE], F32R)
        hn = sb("hn", [P, NBM, L])
        hhi = sb("hhi", [P, 2, CH, NTM], F32R)
        hlo = sb("hlo", [P, 2, CH, NTM], F32R)
        sg = sb("sg", [P, NTM])
        tw = sb("tw", [P, NTM])
        av = sb("av", [P, RING, NTM])
        ahi = sb("ahi", [P, RING, NTM], F32R)
        alo = sb("alo", [P, RING, NTM], F32R)
        ident = sb("ident", [P, P])
        selcol = sb("selcol", [P, E])
        sel = sb("sel", [P, P], F32R)
        rraw = sb("rraw", [P, CH * E])
        router_w = sb("router_w", [P, CH, 2 * E], F32R)
        bias = sb("bias", [P, E])
        stats = sb("stats", [P, NBM, 6])
        mv = sb("mv", [P, 2 * B, 2])
        veps = sb("veps", [P, 2 * B])
        mhalf = sb("mhalf", [P, B])
        rstd = sb("rstd", [P, 2 * B])
        nbias = sb("nbias", [P, 2 * B])
        logits = sb("logits", [P, NBM, E])
        score = sb("score", [P, NBM, E])
        choice = sb("choice", [P, NBM, SCW])
        left = sb("left", [P, NBM, SCW])
        top = sb("top", [P, NBM, 8])
        chosen = sb("chosen", [P, NBM, E])
        wts = sb("wts", [P, NBM, E])
        tot = sb("tot", [P, NBM])
        tinv = sb("tinv", [P, NBM])
        comb = sb("comb", [P, NBM, P], F32R)
        combT = sb("combT", [P, NTM], F32R)
        act_scratch = sb("act_scratch", [P, B])
        flip = sb("flip", [P, P])
        dcol = sb("dcol", [P, HEADS])

        acc = [ctx.enter_context(nc.psum_tensor(f"acc{c}", [P, 512], F32)) for c in range(CH)]
        G = ctx.enter_context(nc.psum_tensor("G", [P, 512], F32))
        U = ctx.enter_context(nc.psum_tensor("U", [P, 512], F32))
        CB = ctx.enter_context(nc.psum_tensor("CB", [P, 512], F32))
        C = [ctx.enter_context(nc.psum_tensor(f"C{i}", [P, 512], F32)) for i in range(3)]

        cw_dram = nc.dram_tensor("combine_rows", (NG, E, NTM), F32, kind="Internal")
        toep_dram = nc.dram_tensor("toep_rows", (HEADS, P + L), F32, kind="Internal")

        s_k = sem("kernel_rows_loaded")
        s_kd = sem("kernel_rows_with_d")
        s_kout = sem("kernel_rows_stored")
        s_toep0 = sem("toeplitz_block0_loaded")
        s_toep1 = sem("toeplitz_block1_loaded")
        s_toep = sem("toeplitz_rest_loaded")
        s_ddiag = sem("d_diagonals_ready")
        s_tdiag = sem("toeplitz_block0_with_d")
        s_ctx = [sem(f"ctx_loaded{g}") for g in range(NG)]
        s_x = [sem(f"x_loaded{g}") for g in range(NG)]
        s_xT = [sem(f"xT_loaded{g}") for g in range(NG)]
        s_dcol = sem("d_loaded")
        s_router = sem("router_loaded")
        s_bias = sem("bias_loaded")
        s_w = [sem(f"weights_loaded{i}") for i in range(3)]
        s_const = sem("constants_ready")
        s_cstep = sem("constants_step")
        s_cinit = sem("combine_buffers_filled")
        s_chain = sem("vector_chain")
        s_rhi = sem("router_hi")
        s_rlo = sem("router_lo")
        s_var = sem("variances_ready")
        s_rstd = sem("rstd_ready")
        s_nb = sem("norm_bias_ready")
        s_norm = sem("rows_normalised")
        s_qn = sem("query_rows_normalised")
        s_qtp = sem("queries_transposed")
        s_q = sem("queries_ready")
        s_q1 = sem("queries_second_half_ready")
        s_kv0 = sem("kv_block0_vector_part")
        s_kv = sem("kv_ready")
        s_sq = sem("squares_ready")
        s_tw = sem("block_toeplitz_ready")
        s_conv = sem("heads_convolved")
        s_y = sem("heads_evacuated")
        s_terms = sem("terms_formed")
        s_pterms = sem("pool_terms_formed")
        s_two = sem("two_sums_left")
        s_xsum = sem("x1_summed")
        s_x1f = sem("x1_of_first_blocks_ready")
        s_zp = sem("pool_terms_added")
        s_sum = sem("terms_sum_step")
        s_x1 = sem("attention_added")
        s_xn = sem("x1_transposed")
        s_htp = sem("h_transposed")
        s_hh = sem("h_hi")
        s_hl = sem("h_lo")
        s_lg = sem("logits_ready")
        s_lsum = sem("logits_summed")
        s_sc = sem("scores_ready")
        s_cx = sem("combine_ready")
        s_ctp = sem("combine_transposed")
        s_comb = sem("combine_in_place")
        s_wgh = sem("gate_up_hi")
        s_wgl = sem("gate_up_lo")
        s_wdh = sem("down_hi")
        s_wdl = sem("down_lo")
        s_sel = sem("select_ready")
        s_spr = sem("combine_spread")
        s_cwt = sem("combine_rows_ready")
        s_cst = sem("combine_rows_stored")
        s_cw = [sem(f"combine_row_on_all_partitions{r}") for r in range(RING)]
        s_g = sem("gate_ready")
        s_u = sem("up_ready")
        s_silu = sem("silu_ready")
        s_t = sem("weighted_silu_ready")
        s_a = sem("act_ready")
        s_ah = sem("act_hi")
        s_al = sem("act_lo")
        s_a_last = sem("last_act_half_ready")
        s_ah_last = sem("last_act_half_hi")
        s_al_last = sem("last_act_lo")
        s_acc = sem("group_accumulated")
        s_res = sem("result_ready")
        s_out = sem("result_stored")

        kdram = toep_dram.ap()
        block = ctx.enter_context(nc.Block())

        def gsl(g):
            return slice(B0[g] * CH, (B0[g] + GROUPS[g]) * CH)

        def lncols(i):
            return (4 * i, NBM) if i < 2 else (6 + i, 1) if i < 6 else (12, NBM)

        def wcols(s, first, n):
            return wraw[:, bass.ds(s * WE + first, n)]

        def toeplitz_rows(rows, h0, h1):
            return bass.AP(rows.tensor, rows.offset + h0 * (P + L) + 1, [[1, P], [P + L, h1 - h0], [1, L]])

        toep_h = toep[:, :].rearrange("p (h l) -> p h l", h=HEADS)

        d_diag = Z[:, 1, 0:2, :].rearrange("p e (h n) -> p (e h) n", n=P)

        def conv_bank(h):
            return (C[0], C[1], C[2], CB)[h]

        def routed_bank(g):
            return G if g else C[1]

        def routed_up_bank(g):
            return U if g else C[0]

        def idle_bank(h):
            return (CB, U)[h % 2]

        def xn_bank(k):
            return (G, U, C[1], C[2])[k]

        def x1_row(b):
            return C[b // 2][:, (b % 2) * L:(b % 2 + 1) * L]

        CW0 = 2 * E
        cw_rows = xnat[CW0:CW0 + E, B - 2:B, :].rearrange("p b l -> p (b l)")

        def cw_all(r):
            return xnat[:, 2 * r:2 * r + 2, :].rearrange("p b l -> p (b l)")

        x1_first = x1T[:, gsl(0), :].rearrange("p (k c) n -> p k c n", c=CH)

        def result_part(t, g, c):
            return t[:, gsl(g), :].rearrange("p (a c) n -> p c a n", c=CH)[:, c]

        def query_half(g, a):
            return qT[:, gsl(g), :].rearrange("p (a c) n -> p a (c n)", a=2)[:, a, :]

        TERMS = [(d, d, 0, d) for d in range(HD)] + [(d, HD - d, d, 0) for d in range(1, HD)]

        def terms(tt, g, k, buf, first, last):
            y = Y[:, buf].rearrange("p h (c n) -> p h c n", n=PAIRS)
            q = qT[:, gsl(g), bass.ds(k * BC, BC)].rearrange("p c (h i) -> p h c i", i=HD)
            z = Z[:, buf].rearrange("p e (c h j) -> p e h c j", h=HB, j=HD)
            for d, e, qi, zj in TERMS[first:last]:
                ins = tt(z[:, e, :, :, zj:zj + HD - d], y[:, :, :, PAIR_AT[d]:PAIR_AT[d] + HD - d],
                         q[:, :, :, qi:qi + HD - d], ALU.mult)
            return ins

        @block.sync
        def _(sp):
            sp.dma_start(xnat[:, 0:NBM, :], x_nat[0:NBM].rearrange("b p l -> p b l")).then_inc(s_x[0], 16)
            sp.dma_start(ctxT[:, gsl(0), :], ctx_t[:, gsl(0), :]).then_inc(s_ctx[0], 16)
            sp.dma_start(toep_h[:, 0:HB, :], toeplitz_rows(kpad, 0, HB)).then_inc(s_toep0, 16)
            sp.dma_start(xnat[:, NBM:B, :], x_nat[NBM:B].rearrange("b p l -> p b l")).then_inc(s_x[1], 16)
            sp.wait_ge(s_kd, 1)
            sp.dma_start(kdram, krow[:, :]).then_inc(s_kout, 16)
            sp.dma_start(x1T[:, gsl(0), :], x_t[:, gsl(0), :]).then_inc(s_xT[0], 16)
            sp.wait_ge(s_kout, 16)
            sp.dma_start(toep_h[:, HB:2 * HB, :], toeplitz_rows(kdram, HB, 2 * HB)).then_inc(s_toep1, 16)
            sp.dma_start(toep_h[:, 2 * HB:HEADS, :], toeplitz_rows(kdram, 2 * HB, HEADS)).then_inc(s_toep, 16)
            for i, (a, b) in enumerate(((0, 1), (1, 3), (3, STEPS))):
                if i == 2:
                    sp.dma_start(ctxT[:, gsl(1), :], ctx_t[:, gsl(1), :]).then_inc(s_ctx[1], 16)
                sp.dma_start(wraw[:, a * WE:b * WE], w_all[:, a * WE:b * WE]).then_inc(s_w[i], 16)
            sp.dma_start(x1T[:, gsl(1), :], x_t[:, gsl(1), :]).then_inc(s_xT[1], 16)

            def combine_row(g, e, r):
                row = cw_dram.ap()[g, bass.ds(e, 1), :].to_broadcast([P, NTM])
                sp.dma_start(cw_all(r), row).then_inc(s_cw[r], 16)

            for g in range(NG):
                n0 = g * STEPS
                sp.wait_ge(s_cwt, g + 1)
                sp.dma_start(cw_dram.ap()[g], cw_rows).then_inc(s_cst, 16)
                sp.wait_ge(s_cst, 16 * (g + 1))
                for s in range(2, 2 + RING):
                    if g:
                        sp.wait_ge(s_a, n0 + s - RING + 1)
                    combine_row(g, s - 1, (n0 + s) % RING)
                if g:
                    for c in range(CH):
                        sp.wait_ge(s_res, CH * (g - 1) + c + 1)
                        sp.dma_start(result_part(out_t, g - 1, c), result_part(x1T, g - 1, c)).then_inc(s_out, 16)
                with sp.Fori(0, (STEPS - 2 - RING) // RING) as k:
                    for j in range(RING):
                        s = 2 + RING + j
                        sp.wait_ge(s_a, k * RING + (n0 + s - RING + 1))
                        combine_row(g, k * RING + (s - 1), (n0 + s) % RING)
            for c in range(CH):
                sp.wait_ge(s_res, CH * (NG - 1) + c + 1)
                sp.dma_start(result_part(out_t, NG - 1, c), result_part(x1T, NG - 1, c)).then_inc(s_out, 16)
            sp.wait_ge(s_out, 16 * CH * NG)

        @block.gpsimd
        def _(pool):
            tt = nc.gpsimd.tensor_tensor

            def rsqrt(i):
                pool.wait_ge(s_var, i + 1)
                c, n = lncols(i)
                tt(rstd[:, c:c + n], veps[:, c:c + n], mhalf[:, 0:n], ALU.pow).then_inc(s_rstd, 1)

            def kv_block(g, k, buf, first=0, last=HD):
                x = ctxT[:, gsl(g), bass.ds(k * BC, BC)].rearrange("p c (h i) -> p h c i", i=HD)
                dst = kv[:, buf, :, :].rearrange("p h (c n) -> p h c n", n=PAIRS)
                for d in range(first, last):
                    ins = tt(dst[:, :, :, PAIR_AT[d]:PAIR_AT[d] + HD - d], x[:, :, :, 0:HD - d],
                             x[:, :, :, d:HD], ALU.mult)
                if last == HD:
                    ins.then_inc(s_kv, 1)

            def pool_terms(k):
                pool.wait_ge(s_y, HB * (k + 1))
                if k >= 2:
                    pool.wait_ge(s_xsum, k - 1)
                terms(tt, 0, k, k % 2, HD, HD + POOL_TERMS).then_inc(s_pterms, 1)

            def add_half(k):
                pool.wait_ge(s_terms, k + 1)
                pool.wait_ge(s_pterms, k)
                z = Z[:, k % 2]
                tt(z[:, 0:2, :], z[:, 0:2, :], z[:, 4:6, :], ALU.add).then_inc(s_zp, 1)

            def gate_up_lo(n, r, s):
                pool.wait_ge(s_wgh, n + 1)
                tt(wlo[:, r, 0:GU], wcols(s, 0, GU), whi[:, r, 0:GU].bitcast(F32), ALU.subtract).then_inc(s_wgl, 1)

            def act_lo(g, n, r):
                pool.wait_ge(s_ah, n + 1)
                nt = GROUPS[g] * P
                tt(alo[:, r, 0:nt], av[:, r, 0:nt], ahi[:, r, 0:nt].bitcast(F32), ALU.subtract).then_inc(s_al, 1)

            nc.gpsimd.memset(mhalf[:, :], -0.5).then_inc(s_cstep, 1)
            nc.gpsimd.memset(ident[:, :], 0.0).then_inc(s_cstep, 1)
            nc.gpsimd.memset(selcol[:, :], 0.0).then_inc(s_cstep, 1)
            nc.gpsimd.memset(flip[:, :], 0.0).then_inc(s_cstep, 1)
            pool.wait_ge(s_cstep, 4)
            nc.gpsimd.affine_select(out=flip[:, :], in_=flip[:, :], compare_op=ALU.not_equal, fill=1.0,
                                    base=1 - P, pattern=[[1, P]], channel_multiplier=1).then_inc(s_const, 1)
            nc.gpsimd.affine_select(out=ident[:, :], in_=ident[:, :], compare_op=ALU.not_equal, fill=1.0,
                                    base=0, pattern=[[-1, P]], channel_multiplier=1).then_inc(s_const, 1)
            nc.gpsimd.affine_select(out=selcol[:, :], in_=selcol[:, :], compare_op=ALU.not_equal, fill=1.0,
                                    base=0, pattern=[[-1, E]], channel_multiplier=1).then_inc(s_cstep, 1)
            pool.wait_ge(s_cstep, 5)
            nc.gpsimd.affine_select(out=selcol[:, :], in_=selcol[:, :], compare_op=ALU.not_equal, fill=1.0,
                                    base=-E, pattern=[[-1, E]], channel_multiplier=1).then_inc(s_const, 1)
            pool.wait_ge(s_ctx[0], 16)
            rsqrt(0)
            kv_block(0, 0, 0, KV0)
            kv_block(0, 1, 1, 1)
            rsqrt(1)
            for k in range(2, BLOCKS):
                pool.wait_ge(s_conv, HB * (k - 1))
                kv_block(0, k, k % 2, 1)
                if k == 2:
                    pool_terms(1)
            add_half(1)
            rsqrt(2)
            pool.wait_ge(s_ctx[1], 16)
            pool.wait_ge(s_conv, HB * 3)
            kv_block(1, 0, 0, 1, 4)
            pool_terms(2)
            add_half(2)
            rsqrt(3)
            pool_terms(3)
            kv_block(1, 0, 0, 4)
            add_half(3)
            rsqrt(4)
            gate_up_lo(0, 0, 0)
            rsqrt(5)
            gate_up_lo(1, 1, 1)
            for g in range(NG):
                n0 = g * STEPS
                nxt = g + 1 < NG
                gate_up_lo(n0 + 2, (n0 + 2) % RING, 2)
                act_lo(g, n0, n0 % RING)

                def lo_parts(n, n_at, s):
                    gate_up_lo(n + 2, (n_at + 2) % RING, s + 2)
                    act_lo(g, n, n_at % RING)

                def turn(k, rest, first):
                    for j in range(LOOP_E):
                        n = n0 + 2 + j
                        lo_parts(k * LOOP_E + n, n, k * LOOP_E + (2 + j))
                        if rest and j == 0:
                            kv_block(g + 1, k + 1, 0, first=KVJ)
                        if first and j == 2:
                            pool.wait_ge(s_conv, k * HB + HB * (BLOCKS + 2))
                            kv_block(g + 1, k + 2, 0, last=KVJ)

                lo_parts(n0 + 1, n0 + 1, 1)
                if nxt:
                    pool.wait_ge(s_conv, HB * (BLOCKS + 1))
                    kv_block(g + 1, 1, 0, last=KVJ)
                with pool.Fori(0, BLOCKS - 2) as k:
                    turn(k, nxt, nxt)
                turn(BLOCKS - 2, nxt, False)
                turn(BLOCKS - 1, False, False)
                for s in range(AFTER, STEPS):
                    n = n0 + s
                    if s + 2 < STEPS or nxt:
                        gate_up_lo(n + 2, (n + 2) % RING, (s + 2) % STEPS)
                    if nxt and s == 14:
                        rsqrt(6)
                    if s + 1 < STEPS or nxt:
                        act_lo(g, n, n % RING)

        @block.scalar
        def _(act):
            def normalise(i, dst, src):
                act.wait_ge(s_nb, i + 1)
                c, n = lncols(i)
                for b in range(n):
                    ins = nc.scalar.activation(dst(b), src(b), ACT.Identity, bias=nbias[:, c + b:c + b + 1],
                                               scale=rstd[:, c + b:c + b + 1])
                ins.then_inc(s_norm, 1)

            def query_rows(g):
                act.wait_ge(s_x[g], 16)
                act.wait_ge(s_nb, g + 1)
                if g:
                    act.wait_ge(s_qtp, 2 * g)
                c, n = lncols(g)
                for b in range(n):
                    ins = nc.scalar.activation(hn[:, b, :], xnat[:, B0[g] + b, :], ACT.Identity,
                                               bias=nbias[:, c + b:c + b + 1], scale=rstd[:, c + b:c + b + 1])
                    if b % 2:
                        ins.then_inc(s_qn, 1)

            def queries(g):
                act.wait_ge(s_qtp, 2 * g + 1)
                ins = nc.scalar.copy(query_half(g, 0), acc[0][:, :])
                if g:
                    act.wait_ge(s_qtp, 2 * g + 2)
                    ins = nc.scalar.copy(query_half(g, 1), acc[1][:, :])
                ins.then_inc(s_q, 1)

            def evacuate(g, k, buf, bank, first=0, last=HB):
                for h in range(first, last):
                    act.wait_ge(s_conv, k * HB + (HB * BLOCKS * g + h + 1))
                    nc.scalar.copy(Y[:, buf, h, :], bank(h)[:, 0:W]).then_inc(s_y, 1)

            def squares(g, k, buf):
                x = ctxT[:, gsl(g), k * BC:(k + 1) * BC].rearrange("p c (h i) -> p h c i", i=HD)
                dst = kv[:, buf, :, :].rearrange("p h (c n) -> p h c n", n=PAIRS)
                nc.scalar.activation(dst[:, :, :, 0:HD], x, ACT.Square).then_inc(s_sq, 1)

            def gate_up_hi(r, s):
                nc.scalar.copy(whi[:, r, 0:GU], wcols(s, 0, GU)).then_inc(s_wgh, 1)

            def down_hi(r, s):
                nc.scalar.copy(whi[:, r, GU:WE], wcols(s, GU, WE - GU)).then_inc(s_wdh, 1)

            def silu(g, n, bank=G):
                act.wait_ge(s_g, n + 1)
                nt = GROUPS[g] * P
                nc.scalar.activation(sg[:, 0:nt], bank[:, 0:nt], ACT.Silu).then_inc(s_silu, 1)

            def act_hi(g, n, r):
                act.wait_ge(s_a, n + 1)
                nt = GROUPS[g] * P
                nc.scalar.copy(ahi[:, r, 0:nt], av[:, r, 0:nt]).then_inc(s_ah, 1)

            def x1_block(k):
                act.wait_ge(s_xsum, k + 1)
                nc.scalar.copy(x1_first[:, k], xn_bank(k)[:, L:2 * L].rearrange("p (c n) -> p c n", c=CH)).then_inc(s_x1f, 1)

            def norm_block(k):
                normalise(2 + k, lambda b: hn[:, 0, :], lambda b: xn_bank(k)[:, 0:L])

            def h_hi_block(k):
                act.wait_ge(s_htp, k + 1)
                nc.scalar.copy(hhi[:, 0, :, k * P:(k + 1) * P],
                               acc[k % 2][:, 0:L].rearrange("p (c n) -> p c n", c=CH)).then_inc(s_hh, 1)

            def scores(g):
                if g:
                    act.wait_ge(s_lsum, g)
                    src = logits[:, :, :]
                else:
                    act.wait_ge(s_lg, 1)
                    src = C[0][:, 0:NBM * E].rearrange("p (b e) -> p b e", e=E)
                nc.scalar.activation(score[:, :, :], src, ACT.Sigmoid).then_inc(s_sc, 1)

            def combine_in_place(g):
                act.wait_ge(s_ctp, g + 1)
                if g:
                    nc.scalar.copy(combT[:, :], C[2][:, :]).then_inc(s_comb, 1)
                    act.wait_ge(s_cst, 16 * g)
                nc.scalar.copy(cw_rows, C[2][CW0:CW0 + E, :]).then_inc(s_cwt, 1)
                if g == 0:
                    nc.scalar.copy(combT[:, :], C[2][:, :]).then_inc(s_comb, 1)

            act.dma_start(dcol[:, :], d_rows).then_inc(s_dcol, 16)
            act.dma_start(krow[:, :], kpad).then_inc(s_k, 16)
            act.dma_start(drow[:, :], dskip).then_inc(s_k, 16)
            act.dma_start(rraw[:, :], router_t).then_inc(s_router, 16)
            act.dma_start(bias[:, :], bias_rows).then_inc(s_bias, 16)
            act.wait_ge(s_const, 1)
            nc.scalar.copy(act_scratch[:, :], mhalf[:, :])
            act.wait_ge(s_ctx[0], 16)
            squares(0, 0, 0)
            squares(0, 1, 1)
            query_rows(0)
            act.wait_ge(s_router, 16)
            nc.scalar.copy(router_w[:, :, 0:E], rraw[:, :].rearrange("p (c e) -> p c e", c=CH)).then_inc(s_rhi, 1)
            queries(0)
            evacuate(0, 0, 0, conv_bank)
            squares(0, 2, 0)
            query_rows(1)
            evacuate(0, 1, 1, conv_bank)
            squares(0, 3, 1)
            queries(1)
            act.wait_ge(s_terms, 1)
            evacuate(0, 2, 0, conv_bank, 0, 2)
            x1_block(0)
            evacuate(0, 2, 0, conv_bank, 2)
            act.wait_ge(s_ctx[1], 16)
            squares(1, 0, 0)
            act.wait_ge(s_terms, 2)
            act.wait_ge(s_pterms, 1)
            evacuate(0, 3, 1, conv_bank, 0, 2)
            norm_block(0)
            x1_block(1)
            evacuate(0, 3, 1, conv_bank, 2)
            h_hi_block(0)
            act.wait_ge(s_w[0], 16)
            gate_up_hi(0, 0)
            down_hi(0, 0)
            norm_block(1)
            x1_block(2)
            h_hi_block(1)
            act.wait_ge(s_terms, 3)
            act.wait_ge(s_pterms, 2)
            evacuate(1, 0, 0, idle_bank, 0, 2)
            norm_block(2)
            evacuate(1, 0, 0, idle_bank, 2)
            h_hi_block(2)
            act.wait_ge(s_w[1], 16)
            gate_up_hi(1, 1)
            norm_block(3)
            h_hi_block(3)
            scores(0)
            for g in range(NG):
                n0 = g * STEPS
                nxt = g + 1 < NG
                silu(g, n0)
                gate_up_hi((n0 + 2) % RING, 2)
                down_hi((n0 + 1) % RING, 1)
                act_hi(g, n0, n0 % RING)
                silu(g, n0 + 1, routed_bank(g))
                combine_in_place(g)
                if g == 0:
                    act.wait_ge(s_w[2], 16)
                    act.wait_ge(s_toep, 16)

                def turn(k, conv):
                    for j in range(LOOP_E):
                        n = n0 + 2 + j
                        silu(g, k * LOOP_E + n)
                        gate_up_hi((n + 2) % RING, k * LOOP_E + (4 + j))
                        down_hi((n + 1) % RING, k * LOOP_E + (3 + j))
                        if conv and j == 2:
                            act.wait_ge(s_terms, k + (BLOCKS * (g + 1) + 1))
                            evacuate(g + 1, k + 1, 0, conv_bank)
                        act_hi(g, k * LOOP_E + n, n % RING)
                        if conv and j == 0:
                            nc.scalar.copy(toep_w[:, :, :].rearrange("p h l -> p (h l)"),
                                           toep[:, bass.ds(k * HB * L + HB * L, HB * L)]).then_inc(s_tw, 1)

                gate_up_hi((n0 + 3) % RING, 3)
                down_hi((n0 + 2) % RING, 2)
                act_hi(g, n0 + 1, (n0 + 1) % RING)
                with act.Fori(0, BLOCKS - 1) as k:
                    turn(k, nxt)
                turn(BLOCKS - 1, False)
                for s in range(AFTER, STEPS):
                    n = n0 + s
                    silu(g, n)
                    if s + 2 < STEPS or nxt:
                        gate_up_hi((n + 2) % RING, (s + 2) % STEPS)
                    if s + 1 < STEPS or nxt:
                        down_hi((n + 1) % RING, (s + 1) % STEPS)
                    if s + 1 < STEPS or nxt:
                        act_hi(g, n, n % RING)
                    if nxt and s == 14:
                        normalise(6, lambda b: hn[:, b, :], x1_row)
                    if nxt and s == 15:
                        act.wait_ge(s_htp, BLOCKS + 1)
                        nc.scalar.copy(hhi[:, 1, 0, :], C[2][:, :]).then_inc(s_hh, 1)
                        nc.scalar.copy(hhi[:, 1, 1, :], C[0][:, :]).then_inc(s_hh, 1)
                if nxt:
                    scores(g + 1)
            for i, t in enumerate(TOKEN_HALVES):
                act.wait_ge(s_a_last, i + 1)
                nc.scalar.copy(ahi[:, R_LAST, t], av[:, R_LAST, t]).then_inc(s_ah_last, 1)

        @block.vector
        def _(dve):
            tt = nc.vector.tensor_tensor
            chain = [0]

            def link(ins):
                chain[0] += 1
                ins.then_inc(s_chain, 1)
                dve.wait_ge(s_chain, chain[0])

            def statistics(i, rows):
                c, n = lncols(i)
                for b in range(n):
                    ins = nc.vector.bn_stats(stats[:, b, :], rows(b))
                link(ins)
                for b in range(n):
                    ins = nc.vector.bn_aggr(mv[:, c + b, :], stats[:, b, :])
                link(ins)
                nc.vector.tensor_scalar(veps[:, c:c + n], mv[:, c:c + n, 1], EPS, None,
                                        ALU.add).then_inc(s_var, 1)

            def did(ins):
                chain[0] += 1
                ins.then_inc(s_chain, 1)
                return chain[0]

            def norm_bias(i):
                dve.wait_ge(s_rstd, i + 1)
                c, n = lncols(i)
                nc.vector.scalar_tensor_tensor(out=nbias[:, c:c + n], in0=mv[:, c:c + n, 0], scalar=-1.0,
                                               in1=rstd[:, c:c + n], op0=ALU.mult, op1=ALU.mult).then_inc(s_nb, 1)

            def add_to_x(g, k, buf):
                z = Z[:, buf, 0, :].rearrange("p (b c n) -> p b c n", c=CH, n=BC)
                if g == 0:
                    x = x1_first[:, k].rearrange("p c (b n) -> p c b n", n=BC)
                    z = z.rearrange("p b c n -> p c b n")
                else:
                    x = x1T[:, gsl(g), bass.ds(k * BC, BC)].rearrange("p (b c) n -> p b c n", c=CH)
                tt(x, x, z, ALU.add).then_inc(s_x1, 1)

            def first_terms(k):
                dve.wait_ge(s_y, HB * (k + 1))
                if k >= 2:
                    dve.wait_ge(s_xsum, k - 1)
                if k == 0:
                    ins = terms(tt, 0, k, k % 2, 0, len(TERMS))
                else:
                    terms(tt, 0, k, k % 2, 0, HD)
                    ins = terms(tt, 0, k, k % 2, HD + POOL_TERMS, len(TERMS))
                ins.then_inc(s_terms, 1)

            def first_block(k):
                z = Z[:, k % 2]
                c, _ = lncols(2 + k - 1)

                def add_four():
                    dve.wait_ge(s_terms, k + 1)
                    if k == 0:
                        return did(tt(z[:, 0:4, :], z[:, 0:4, :], z[:, 4:8, :], ALU.add))
                    dve.wait_ge(s_pterms, k)
                    return did(tt(z[:, 2:4, :], z[:, 2:4, :], z[:, 6:8, :], ALU.add))

                if k < BLOCKS:
                    first_terms(k)
                if k == BLOCKS - 1:
                    four = add_four()
                if k >= 1:
                    dve.wait_ge(s_xn, k)
                    seen = did(nc.vector.bn_stats(stats[:, 0, :], xn_bank(k - 1)[:, 0:L]))
                    dve.wait_ge(s_chain, seen)
                    seen = did(nc.vector.bn_aggr(mv[:, c, :], stats[:, 0, :]))
                if k < BLOCKS - 1:
                    four = add_four()
                if k >= 1:
                    dve.wait_ge(s_chain, seen)
                    nc.vector.tensor_scalar(veps[:, c:c + 1], mv[:, c:c + 1, 1], EPS, None, ALU.add).then_inc(s_var, 1)
                if k < BLOCKS:
                    if k >= 1:
                        dve.wait_ge(s_zp, k)
                    dve.wait_ge(s_chain, four)
                    tt(z[:, 0:2, :], z[:, 0:2, :], z[:, 2:4, :], ALU.add).then_inc(s_two, 1)
                if k >= 1:
                    norm_bias(2 + k - 1)
                if k in (BLOCKS - 2, BLOCKS):
                    h_lo_block(k - 2)
                if k == BLOCKS - 1:
                    dve.wait_ge(s_two, BLOCKS)
                    link(tt(z[:, 0, :], z[:, 0, :], z[:, 1, :], ALU.add))
                    add_to_x(0, k, k % 2)
                    h_lo_block(k - 2)

            def next_terms(g, k, first, last):
                return terms(tt, g, k, 0, first, last)

            def next_sums(g, k):
                z = Z[:, 0]
                for i, half in enumerate((4, 2, 1)):
                    if i == 0:
                        dve.wait_ge(s_terms, k + (BLOCKS * g + 1))
                    else:
                        dve.wait_ge(s_sum, 3 * k + (3 * BLOCKS * (g - 1) + i))
                    tt(z[:, 0:half, :], z[:, 0:half, :], z[:, half:2 * half, :], ALU.add).then_inc(s_sum, 1)
                dve.wait_ge(s_sum, 3 * k + (3 * BLOCKS * (g - 1) + 3))
                add_to_x(g, k, 0)

            def down_lo(n, r, s):
                dve.wait_ge(s_wdh, n + 1)
                tt(wlo[:, r, GU:WE], wcols(s, GU, WE - GU), whi[:, r, GU:WE].bitcast(F32),
                   ALU.subtract).then_inc(s_wdl, 1)

            def activations(g, n, r, at, uses=None, last=False, up_bank=U):
                nt = GROUPS[g] * P
                dve.wait_ge(s_silu, n + 1)
                gate = sg
                if at is not None:
                    if uses is None:
                        dve.wait_ge(s_spr, g + 1)
                        weights = CB[:, 0:nt]
                    else:
                        dve.wait_ge(s_cw[r], uses)
                        weights = cw_all(r)[:, 0:nt]
                    tt(tw[:, 0:nt], sg[:, 0:nt], weights, ALU.mult).then_inc(s_t, 1)
                    dve.wait_ge(s_t, at + 1)
                    gate = tw
                dve.wait_ge(s_u, n + 1)
                if last:
                    for t in TOKEN_HALVES:
                        tt(av[:, r, t], gate[:, t], up_bank[:, t], ALU.mult).then_inc(s_a_last, 1)
                else:
                    tt(av[:, r, 0:nt], gate[:, 0:nt], up_bank[:, 0:nt], ALU.mult).then_inc(s_a, 1)

            def loaded(g, s):
                return 16 * (ROWS * g + (s - 2) // RING + 1)

            def h_lo_block(k):
                dve.wait_ge(s_hh, k + 1)
                tt(hlo[:, 0, :, k * P:(k + 1) * P], acc[k % 2][:, 0:L].rearrange("p (c n) -> p c n", c=CH),
                   hhi[:, 0, :, k * P:(k + 1) * P].bitcast(F32), ALU.subtract).then_inc(s_hl, 1)

            def sum_logits(g, bank):
                dve.wait_ge(s_lg, g + 1)
                parts = bank[:, 0:NBM * 2 * E].rearrange("p (b i e) -> p b i e", i=2, e=E)
                link(nc.vector.tensor_copy(logits[:, :, :], parts[:, :, 0, :]))
                tt(logits[:, :, :], logits[:, :, :], parts[:, :, 1, :], ALU.add).then_inc(s_lsum, 1)

            def combine(g):
                n = GROUPS[g]
                dve.wait_ge(s_sc, g + 1)
                dve.wait_ge(s_cinit, 2)
                link(tt(choice[:, 0:n, 0:E], score[:, 0:n, :],
                        bias[:, :].unsqueeze(1).to_broadcast([P, n, E]), ALU.add))
                for b in range(n):
                    ins = nc.vector.max(top[:, b, :], choice[:, b, 0:E])
                link(ins)
                link(nc.vector.memset(top[:, 0:n, TOPK:8], SENT))
                for b in range(n):
                    ins = nc.vector.match_replace(out=left[:, b, :], in_to_replace=top[:, b, :],
                                                  in_values=choice[:, b, :], imm_value=TAKEN)
                link(ins)
                link(tt(chosen[:, 0:n, :], choice[:, 0:n, 0:E], left[:, 0:n, 0:E], ALU.not_equal))
                link(tt(wts[:, 0:n, :], score[:, 0:n, :], chosen[:, 0:n, :], ALU.mult))
                summed = did(nc.vector.tensor_reduce(tot[:, 0:n], wts[:, 0:n, :], AX_X, ALU.add))
                activations(g, g * STEPS, g * STEPS % RING, None)
                dve.wait_ge(s_chain, summed)
                link(nc.vector.tensor_scalar(tot[:, 0:n], tot[:, 0:n], 1e-20, None, ALU.add))
                link(nc.vector.reciprocal(tinv[:, 0:n], tot[:, 0:n]))
                inverse = tinv[:, 0:n].unsqueeze(2).to_broadcast([P, n, E])
                whole = comb[:, 0:n, CW0:CW0 + E].bitcast(F32)
                tt(whole, wts[:, 0:n, :], inverse, ALU.mult)
                link(tt(comb[:, 0:n, 0:E], wts[:, 0:n, :], inverse, ALU.mult))
                tt(comb[:, 0:n, E:2 * E], whole, comb[:, 0:n, 0:E].bitcast(F32),
                   ALU.subtract).then_inc(s_cx, 1)

            def result(g):
                for c in range(CH):
                    dve.wait_ge(s_acc, CH * g + c + 1)
                    if g == 0:
                        x = x1_first[:, :, c, :]
                        y = acc[c][:, :].rearrange("p (k n) -> p k n", k=BLOCKS)
                    else:
                        x = x1T[:, gsl(g), :].rearrange("p (b c) n -> p c b n", c=CH)[:, c]
                        y = acc[c][:, :].rearrange("p (b n) -> p b n", n=P)
                    tt(x, y, x, ALU.add).then_inc(s_res, 1)

            nc.vector.memset(comb[:, :, :].bitcast(F32), 0.0).then_inc(s_cinit, 1)
            nc.vector.memset(choice[:, :, :], SENT).then_inc(s_cinit, 1)
            dve.wait_ge(s_x[0], 16)
            statistics(0, lambda b: xnat[:, b, :])
            dve.wait_ge(s_dcol, 16)
            dve.wait_ge(s_const, 1)
            tt(d_diag, flip[:, :].unsqueeze(1).to_broadcast([P, HB, P]),
               dcol[:, 0:HB].unsqueeze(2).to_broadcast([P, HB, P]), ALU.mult).then_inc(s_ddiag, 1)
            dve.wait_ge(s_ctx[0], 16)
            x = ctxT[:, gsl(0), 0:BC].rearrange("p c (h i) -> p h c i", i=HD)
            dst = kv[:, 0, :, :].rearrange("p h (c n) -> p h c n", n=PAIRS)
            for d in range(1, KV0):
                ins = tt(dst[:, :, :, PAIR_AT[d]:PAIR_AT[d] + HD - d], x[:, :, :, 0:HD - d], x[:, :, :, d:HD], ALU.mult)
                if d == 1:
                    dve.wait_ge(s_k, 32)
                    tt(krow[:, P:P + 1], krow[:, P:P + 1], drow[:, :], ALU.add).then_inc(s_kd, 1)
                    norm_bias(0)
            ins.then_inc(s_kv0, 1)
            dve.wait_ge(s_toep0, 16)
            dve.wait_ge(s_ddiag, 1)
            tt(toep_h[:, 0:HB, 0:P], toep_h[:, 0:HB, 0:P], d_diag, ALU.add).then_inc(s_tdiag, 1)
            dve.wait_ge(s_x[1], 16)
            statistics(1, lambda b: xnat[:, NBM + b, :])
            dve.wait_ge(s_rhi, 1)
            tt(router_w[:, :, E:2 * E], rraw[:, :].rearrange("p (c e) -> p c e", c=CH),
               router_w[:, :, 0:E].bitcast(F32), ALU.subtract).then_inc(s_rlo, 1)
            dve.wait_ge(s_qtp, 2)
            nc.vector.tensor_copy(query_half(0, 1), acc[1][:, :]).then_inc(s_q1, 1)
            norm_bias(1)
            dve.wait_ge(s_q1, 1)
            dve.wait_ge(s_q, 1)
            dve.wait_ge(s_xT[0], 16)
            for k in range(BLOCKS + 1):
                first_block(k)
            dve.wait_ge(s_w[0], 16)
            down_lo(0, 0, 0)
            dve.wait_ge(s_bias, 16)
            dve.wait_ge(s_const, 3)
            nc.vector.tensor_copy(sel[:, :], selcol[:, 0:1].to_broadcast([P, P])).then_inc(s_sel, 1)
            h_lo_block(BLOCKS - 1)
            combine(0)
            for g in range(NG):
                n0 = g * STEPS
                nxt = g + 1 < NG
                down_lo(n0 + 1, (n0 + 1) % RING, 1)
                if g:
                    result(g - 1)
                if nxt:
                    dve.wait_ge(s_q, g + 2)
                    dve.wait_ge(s_xT[g + 1], 16)
                activations(g, n0 + 1, (n0 + 1) % RING, g * E, up_bank=routed_up_bank(g))
                down_lo(n0 + 2, (n0 + 2) % RING, 2)

                def turn(k):
                    for j in range(LOOP_E):
                        n = n0 + 2 + j
                        activations(g, k * LOOP_E + n, n % RING, k * LOOP_E + (g * E + 1 + j), k * 16 + loaded(g, 2 + j))
                        down_lo(k * LOOP_E + (n + 1), (n + 1) % RING, k * LOOP_E + (3 + j))
                        if nxt and j == 0:
                            dve.wait_ge(s_y, k * HB + (HB * BLOCKS * (g + 1) + HB))
                            dve.wait_ge(s_x1, k + 1)
                            next_terms(g + 1, k, 0, 7)
                        if nxt and j == 1:
                            next_terms(g + 1, k, 7, len(TERMS)).then_inc(s_terms, 1)
                            next_sums(g + 1, k)

                with dve.Fori(0, BLOCKS) as k:
                    turn(k)
                for s in range(AFTER, STEPS):
                    n = n0 + s
                    if nxt and s == 14:
                        dve.wait_ge(s_xn, BLOCKS + 1)
                        statistics(6, x1_row)
                    activations(g, n, n % RING, g * E + s - 1, loaded(g, s), not nxt and s == STEPS - 1)
                    if s + 1 < STEPS or nxt:
                        down_lo(n + 1, (n + 1) % RING, (s + 1) % STEPS)
                    if nxt and s == 14:
                        norm_bias(6)
                    if nxt and s == 15:
                        for c, src in enumerate((C[2], C[0])):
                            dve.wait_ge(s_hh, BLOCKS + c + 1)
                            ins = tt(hlo[:, 1, c, :], src[:, :], hhi[:, 1, c, :].bitcast(F32), ALU.subtract)
                        ins.then_inc(s_hl, 1)
                if nxt:
                    sum_logits(g + 1, C[1])
                    combine(g + 1)
            for i, t in enumerate(TOKEN_HALVES):
                dve.wait_ge(s_ah_last, i + 1)
                tt(alo[:, R_LAST, t], av[:, R_LAST, t], ahi[:, R_LAST, t].bitcast(F32),
                   ALU.subtract).then_inc(s_al_last, 1)
            result(NG - 1)

        @block.tensor
        def _(pe):
            mm = nc.tensor.matmul

            def keep_busy(n, bank):
                for i in range(n):
                    nc.tensor.transpose(bank[:, 0:P], ident[:, :], ident[:, :])

            def queries(g, a):
                pe.wait_ge(s_qn, 2 * g + a + 1)
                if g:
                    pe.wait_ge((s_q, s_q1)[a], g)
                for b in (2 * a, 2 * a + 1):
                    for c in range(CH):
                        at = (b % 2) * L + c * P
                        ins = nc.tensor.transpose(acc[a][:, at:at + P], hn[:, b, c * P:(c + 1) * P], ident[:, :])
                ins.then_inc(s_qtp, 1)

            def convolve(g, h, buf, out, matrices):
                m = kv[:, buf, h, :].rearrange("p (b c n) -> p b c n", c=CH, n=PAIRS)
                y = out[:, 0:W].rearrange("p (b c n) -> p b c n", c=CH, n=PAIRS)
                near, far = matrices[:, 0:P], matrices[:, P:L]
                mm(y[:, :, 0, :], near, m[:, :, 0, :], start=True, stop=True)
                mm(y[:, :, 1, :], near, m[:, :, 1, :], start=True, stop=False)
                mm(y[:, :, 1, :], far, m[:, :, 0, :], start=False, stop=True).then_inc(s_conv, 1)

            def convolve_first(k, first=0, last=HB):
                pe.wait_ge(s_kv, k + 1)
                pe.wait_ge(s_sq, k + 1)
                for h in range(first, last):
                    if k:
                        pe.wait_ge(s_y, HB * (k - 1) + h + 1)
                    convolve(0, h, k % 2, conv_bank(h), toep_h[:, HB * k + h, :])

            def sum_block(k):
                pe.wait_ge(s_two, k + 1)
                if k == 0:
                    pe.wait_ge(s_xT[0], 16)
                out = xn_bank(k)[:, L:2 * L].rearrange("p (c b n) -> p c b n", c=CH, n=BC)
                z = [Z[:, k % 2, e, :].rearrange("p (b c n) -> p c b n", c=CH, n=BC) for e in range(2)]
                x = x1_first[:, k].rearrange("p c (b n) -> p c b n", n=BC)
                mm(out, ident[:, :], x, start=True, stop=False)
                mm(out, ident[:, :], z[0], start=False, stop=False)
                mm(out, ident[:, :], z[1], start=False, stop=True).then_inc(s_xsum, 1)

            def x1_rows_block(k):
                if k < BLOCKS - 1:
                    pe.wait_ge(s_x1f, k + 1)
                else:
                    pe.wait_ge(s_x1, 1)
                for c in range(CH):
                    ins = nc.tensor.transpose(xn_bank(k)[:, c * P:(c + 1) * P], x1_first[:, k, c, :], ident[:, :])
                ins.then_inc(s_xn, 1)

            def h_block(k):
                pe.wait_ge(s_norm, k + 1)
                if k == 0:
                    pe.wait_ge(s_q, NG)
                if k >= 2:
                    pe.wait_ge(s_hl, k - 1)
                for c in range(CH):
                    ins = nc.tensor.transpose(acc[k % 2][:, c * P:(c + 1) * P], hn[:, 0, c * P:(c + 1) * P],
                                              ident[:, :])
                ins.then_inc(s_htp, 1)

            def product3(out, whi_, wlo_, xhi, xlo, start, stop):
                mm(out, whi_, xhi, start=start, stop=False, skip_group_check=True)
                mm(out, whi_, xlo, start=False, stop=False, skip_group_check=True)
                return mm(out, wlo_, xhi, start=False, stop=stop, skip_group_check=True)

            def router_first(b, lo_count=None):
                out = C[0][:, b * E:(b + 1) * E]
                for c in range(CH):
                    h = hhi[:, 0, c, b * P:(b + 1) * P]
                    mm(out, h, router_w[:, c, 0:E], start=(c == 0), stop=False)
                    mm(out, h, router_w[:, c, E:2 * E], start=False, stop=False)
                if lo_count is not None:
                    pe.wait_ge(s_hl, lo_count)
                for c in range(CH):
                    ins = mm(out, hlo[:, 0, c, b * P:(b + 1) * P], router_w[:, c, 0:E], start=False,
                             stop=(c == CH - 1))
                return ins

            def router(g, b, bank):
                at = b * 2 * E
                for c in range(CH):
                    h1, h2 = (t[:, g % 2, c, b * P:(b + 1) * P] for t in (hhi, hlo))
                    mm(bank[:, at:at + 2 * E], h1, router_w[:, c, :], start=(c == 0), stop=False,
                       skip_group_check=True)
                    ins = mm(bank[:, at:at + E], h2, router_w[:, c, 0:E], start=False, stop=(c == CH - 1),
                             skip_group_check=True)
                return ins

            def combine_turned(g):
                pe.wait_ge(s_cx, g + 1)
                for b in range(GROUPS[g]):
                    ins = nc.tensor.transpose(C[2][:, b * P:(b + 1) * P], comb[:, b, :].bitcast(F32), ident[:, :])
                ins.then_inc(s_ctp, 1)

            def spread(g):
                pe.wait_ge(s_comb, g + 1)
                pe.wait_ge(s_sel, 1)
                if g:
                    pe.wait_ge(s_t, (g - 1) * E + 1)
                mm(CB[:, 0:GROUPS[g] * P], sel[:, :], combT[:, 0:GROUPS[g] * P], start=True,
                   stop=True).then_inc(s_spr, 1)

            def hidden(g, r, half, out, t=slice(0, NTM)):
                for c in range(CH):
                    at = (2 * half + c) * P
                    ins = product3(out[:, t], whi[:, r, at:at + P], wlo[:, r, at:at + P],
                                   hhi[:, g % 2, c, t], hlo[:, g % 2, c, t], c == 0, c == CH - 1)
                return ins

            def gate(g, n, r, bank=G):
                pe.wait_ge(s_wgl, n + 1)
                hidden(g, r, 0, bank).then_inc(s_g, 1)

            def up(g, r, bank=U):
                hidden(g, r, 1, bank).then_inc(s_u, 1)

            def down(g, n, r, first=False, last=False, with_spread=False):
                nt = GROUPS[g] * P
                pe.wait_ge(s_ah, n + 1)
                pe.wait_ge(s_wdl, n + 1)
                chunk = [slice(GU + c * P, GU + (c + 1) * P) for c in range(CH)]
                for c in range(CH):
                    mm(acc[c][:, 0:nt], whi[:, r, chunk[c]], ahi[:, r, 0:nt], start=first, stop=False,
                       skip_group_check=True)
                    mm(acc[c][:, 0:nt], wlo[:, r, chunk[c]], ahi[:, r, 0:nt], start=False, stop=False,
                       skip_group_check=True)
                if with_spread:
                    spread(g)
                pe.wait_ge(s_al, n + 1)
                for c in range(CH):
                    ins = mm(acc[c][:, 0:nt], whi[:, r, chunk[c]], alo[:, r, 0:nt], start=False, stop=last,
                             skip_group_check=True)
                    if last:
                        ins.then_inc(s_acc, 1)

            def down_last():
                def part(c, w, x, t, stop=False):
                    return mm(acc[c][:, t], w[:, R_LAST, GU + c * P:GU + (c + 1) * P], x[:, R_LAST, t], start=False,
                              stop=stop, skip_group_check=True)
                pe.wait_ge(s_wdl, NG * STEPS)
                for i, t in enumerate(TOKEN_HALVES):
                    pe.wait_ge(s_ah_last, i + 1)
                    part(0, whi, ahi, t)
                    part(0, wlo, ahi, t)
                    part(1, whi, ahi, t)
                pe.wait_ge(s_al_last, len(TOKEN_HALVES))
                every = slice(0, NTM)
                part(0, whi, alo, every, stop=True).then_inc(s_acc, 1)
                part(1, wlo, ahi, every)
                part(1, whi, alo, every, stop=True).then_inc(s_acc, 1)

            pe.wait_ge(s_const, 3)
            keep_busy(WARM_UP, acc[1])
            queries(0, 0)
            pe.wait_ge(s_kv0, 1)
            pe.wait_ge(s_tdiag, 1)
            convolve_first(0, 0, 2)
            queries(0, 1)
            convolve_first(0, 2)
            pe.wait_ge(s_toep1, 16)
            convolve_first(1)
            queries(1, 0)
            queries(1, 1)
            pe.wait_ge(s_toep, 16)
            convolve_first(2, 0, 2)
            sum_block(0)
            convolve_first(2, 2, 3)
            x1_rows_block(0)
            convolve_first(2, 3)
            convolve_first(3, 0, 2)
            sum_block(1)
            convolve_first(3, 2, 3)
            x1_rows_block(1)
            convolve_first(3, 3)
            h_block(0)
            pe.wait_ge(s_y, HB * BLOCKS)
            keep_busy(13, CB)
            sum_block(2)
            h_block(1)
            x1_rows_block(2)
            pe.wait_ge(s_rlo, 1)
            router_first(0, 1)
            pe.wait_ge(s_kv, BLOCKS + 1)
            pe.wait_ge(s_sq, BLOCKS + 1)
            pe.wait_ge(s_norm, 2)
            for h in range(HB):
                if h >= 2:
                    pe.wait_ge(s_y, HB * BLOCKS + h - 1)
                if h == HB - 1:
                    x1_rows_block(BLOCKS - 1)
                convolve(1, h, 0, idle_bank(h), toep_h[:, h, :])
            h_block(2)
            pe.wait_ge(s_hl, 2)
            router_first(1)
            half_a, half_b = TOKEN_HALVES
            pe.wait_ge(s_wgl, 1)
            hidden(0, 0, 0, G, half_a)
            pe.wait_ge(s_y, HB * BLOCKS + HB)
            hidden(0, 0, 1, U, half_a)
            h_block(3)
            pe.wait_ge(s_hl, 3)
            router_first(2)
            keep_busy(3, CB)
            pe.wait_ge(s_hh, BLOCKS)
            router_first(3, BLOCKS).then_inc(s_lg, 1)
            hidden(0, 0, 0, G, half_b).then_inc(s_g, 1)
            hidden(0, 0, 1, U, half_b).then_inc(s_u, 1)
            for g in range(NG):
                n0 = g * STEPS
                nxt = g + 1 < NG
                if g:
                    pe.wait_ge(s_silu, n0)
                    gate(g, n0, n0 % RING)
                    pe.wait_ge(s_a, n0)
                    up(g, n0 % RING)
                    down(g - 1, n0 - 1, (n0 - 1) % RING, last=True)
                    pe.wait_ge(s_silu, n0 + 1)
                gate(g, n0 + 1, (n0 + 1) % RING, routed_bank(g))
                if g:
                    combine_turned(g)
                    pe.wait_ge(s_a, n0 + 1)
                else:
                    pe.wait_ge(s_sc, 1)
                up(g, (n0 + 1) % RING, routed_up_bank(g))
                if g == 0:
                    combine_turned(g)
                    down(g, n0, n0 % RING, first=True, with_spread=True)
                else:
                    spread(g)
                    pe.wait_ge(s_res, CH * g)
                    down(g, n0, n0 % RING, first=True)

                def turn(k, conv):
                    for j in range(LOOP_E):
                        n = n0 + 2 + j
                        pe.wait_ge(s_silu, k * LOOP_E + n)
                        gate(g, k * LOOP_E + n, n % RING)
                        if conv and j == 2:
                            pe.wait_ge(s_kv, k + (BLOCKS * (g + 1) + 2))
                            pe.wait_ge(s_tw, k + 1)
                            for h in range(HB):
                                convolve(g + 1, h, 0, conv_bank(h), toep_w[:, h, :])
                        pe.wait_ge(s_a, k * LOOP_E + n)
                        up(g, n % RING)
                        down(g, k * LOOP_E + (n - 1), (n - 1) % RING)

                with pe.Fori(0, BLOCKS - 1) as k:
                    turn(k, nxt)
                turn(BLOCKS - 1, False)
                for s in range(AFTER, STEPS):
                    n = n0 + s
                    pe.wait_ge(s_silu, n)
                    gate(g, n, n % RING)
                    if nxt and s == 14:
                        pe.wait_ge(s_x1, 1 + BLOCKS)
                        for b in range(NBM):
                            for c in range(CH):
                                ins = nc.tensor.transpose(x1_row(b)[:, c * P:(c + 1) * P],
                                                          x1T[:, (B0[1] + b) * CH + c, :], ident[:, :])
                        ins.then_inc(s_xn, 1)
                    pe.wait_ge(s_a, n)
                    up(g, n % RING)
                    down(g, n - 1, (n - 1) % RING)
                    if nxt and s == 15:
                        pe.wait_ge(s_norm, BLOCKS + 1)
                        for c, dst in enumerate((C[2], C[0])):
                            for b in range(NBM):
                                ins = nc.tensor.transpose(dst[:, b * P:(b + 1) * P], hn[:, b, c * P:(c + 1) * P],
                                                          ident[:, :])
                        ins.then_inc(s_htp, 1)
                if nxt:
                    pe.wait_ge(s_hl, BLOCKS + 1)
                    for b in range(NBM):
                        ins = router(g + 1, b, C[1])
                    ins.then_inc(s_lg, 1)
            down_last()


def kernel(x, ctx_2048, L0_xattn_ssm_kernel, L0_xattn_D, L0_ffn_router_w, L0_ffn_router_bias,
           L0_ffn_expert_gate_w, L0_ffn_expert_up_w, L0_ffn_expert_down_w, L0_ffn_shared_gate_w,
           L0_ffn_shared_up_w, L0_ffn_shared_down_w):
    import numpy as np
    import concourse.bacc as bacc
    from concourse.bass_utils import run_bass_kernel_spmd

    def positions_first(a):
        return np.ascontiguousarray(np.asarray(a).reshape(B, P, CH, P).transpose(3, 0, 2, 1).reshape(P, B * CH, P))

    def tokens_first(a):
        a = np.asarray(a)
        first = a[:NBM].reshape(NBM, BLOCKS, BC, CH, P).transpose(4, 1, 3, 0, 2).reshape(P, NBM * CH, P)
        second = a[NBM:].reshape(NBM, P, CH, P).transpose(3, 0, 2, 1).reshape(P, NBM * CH, P)
        return np.ascontiguousarray(np.concatenate([first, second], 1))

    def with_shared(shared, experts):
        return np.concatenate([np.asarray(shared)[None], np.asarray(experts)], 0)

    def in_first(w):
        return w.reshape(STEPS, F, CH, P).transpose(3, 0, 2, 1).reshape(P, STEPS, CH * F)

    xs = np.asarray(x)
    gate = in_first(with_shared(L0_ffn_shared_gate_w, L0_ffn_expert_gate_w))
    up = in_first(with_shared(L0_ffn_shared_up_w, L0_ffn_expert_up_w))
    down = with_shared(L0_ffn_shared_down_w, L0_ffn_expert_down_w).transpose(2, 0, 1)
    ker = np.asarray(L0_xattn_ssm_kernel)
    arrays = {
        "kernel_rows": np.ascontiguousarray(np.concatenate([np.zeros((HEADS, P), ker.dtype), ker], 1)),
        "d_skip": np.ascontiguousarray(np.asarray(L0_xattn_D).reshape(HEADS, 1)),
        "d_rows": np.ascontiguousarray(np.broadcast_to(np.asarray(L0_xattn_D), (P, HEADS))),
        "ctx_t": np.ascontiguousarray(positions_first(ctx_2048)[::-1]),
        "x_nat": np.ascontiguousarray(xs),
        "x_t": tokens_first(xs),
        "w_all": np.ascontiguousarray(np.concatenate([gate, up, down], 2).reshape(P, STEPS * WE)),
        "router_t": np.ascontiguousarray(
            np.asarray(L0_ffn_router_w).reshape(E, CH, P).transpose(2, 1, 0).reshape(P, CH * E)),
        "bias_rows": np.ascontiguousarray(np.broadcast_to(np.asarray(L0_ffn_router_bias), (P, E))),
    }
    nc = bacc.Bacc("TRN2", target_bir_lowering=False, num_devices=1)
    args = [nc.dram_tensor(name, a.shape, mybir.dt.from_np(a.dtype), kind="ExternalInput").ap()
            for name, a in arrays.items()]
    out = nc.dram_tensor("out_t", (P, B * CH, P), F32, kind="ExternalOutput").ap()
    build(nc, *args, out)
    r = run_bass_kernel_spmd(nc, [arrays], core_ids=[0])
    got = r.results[0]["out_t"]
    first = got[:, :NBM * CH].reshape(P, BLOCKS, CH, NBM, BC).transpose(3, 1, 4, 2, 0).reshape(NBM, P, L)
    second = got[:, NBM * CH:].reshape(P, NBM, CH, P).transpose(1, 3, 2, 0).reshape(NBM, P, L)
    return np.ascontiguousarray(np.concatenate([first, second], 0))
```
